# Optimizing a Trainium2 kernel written in Bass

```python
import numpy as np
import jax
import jax.numpy as jnp

def _softmax(x, axis=-1):
    return jax.nn.softmax(x, axis=axis)

def _gelu(x):
    return jax.nn.gelu(x, approximate=True)

def _silu(x):
    return jax.nn.silu(x)

def _sigmoid(x):
    return jax.nn.sigmoid(x)

def _layernorm(x, axis=-1, eps=1e-05):
    m = jnp.mean(x, axis=axis, keepdims=True)
    v = jnp.var(x, axis=axis, keepdims=True)
    return (x - m) / jnp.sqrt(v + eps)

def _scatter_add(tgt, idx, src, axis=0):
    return tgt.at[idx].add(src)

def _segment_sum(src, seg, n):
    return jax.ops.segment_sum(src, seg, n)
kernel_name = 'mk_dlrm_tower_d1_rec_r8_d1eba5'

def setup_inputs(seed: int=0):
    np.random.seed(seed)
    _w = jnp.asarray

    def _rec_inputs():
        import jax
        import jax.numpy as jnp
        _tk = jax.random.key(seed)
        dense_ctx = jax.random.normal(jax.random.fold_in(_tk, 190), (1024, 16), jnp.float32)
        ids = jnp.stack([jax.random.randint(jax.random.fold_in(_tk, 200 + f), (1024,), 0, v, jnp.int32) for f, v in enumerate([125000, 125000, 1250, 1250, 1000, 12500, 1000, 1000, 1000, 1250, 12500, 125000, 1250, 12500, 1250, 1000, 1250, 1250, 125000, 125000, 12500, 1000, 1000, 1250, 12500, 12500, 12500, 1250, 1250, 12500, 1250, 125000, 12500, 1250, 1250, 12500, 1000, 1000, 1250])], axis=1)
        tbl_0 = 0.05 * jax.random.normal(jax.random.fold_in(_tk, 500 + 0), (125000, 32), jnp.float32)
        tbl_1 = 0.05 * jax.random.normal(jax.random.fold_in(_tk, 500 + 1), (125000, 32), jnp.float32)
        tbl_2 = 0.05 * jax.random.normal(jax.random.fold_in(_tk, 500 + 2), (1250, 32), jnp.float32)
        tbl_3 = 0.05 * jax.random.normal(jax.random.fold_in(_tk, 500 + 3), (1250, 32), jnp.float32)
        tbl_4 = 0.05 * jax.random.normal(jax.random.fold_in(_tk, 500 + 4), (1000, 32), jnp.float32)
        tbl_5 = 0.05 * jax.random.normal(jax.random.fold_in(_tk, 500 + 5), (12500, 32), jnp.float32)
        tbl_6 = 0.05 * jax.random.normal(jax.random.fold_in(_tk, 500 + 6), (1000, 32), jnp.float32)
        tbl_7 = 0.05 * jax.random.normal(jax.random.fold_in(_tk, 500 + 7), (1000, 32), jnp.float32)
        tbl_8 = 0.05 * jax.random.normal(jax.random.fold_in(_tk, 500 + 8), (1000, 32), jnp.float32)
        tbl_9 = 0.05 * jax.random.normal(jax.random.fold_in(_tk, 500 + 9), (1250, 32), jnp.float32)
        tbl_10 = 0.05 * jax.random.normal(jax.random.fold_in(_tk, 500 + 10), (12500, 32), jnp.float32)
        tbl_11 = 0.05 * jax.random.normal(jax.random.fold_in(_tk, 500 + 11), (125000, 32), jnp.float32)
        tbl_12 = 0.05 * jax.random.normal(jax.random.fold_in(_tk, 500 + 12), (1250, 32), jnp.float32)
        tbl_13 = 0.05 * jax.random.normal(jax.random.fold_in(_tk, 500 + 13), (12500, 32), jnp.float32)
        tbl_14 = 0.05 * jax.random.normal(jax.random.fold_in(_tk, 500 + 14), (1250, 32), jnp.float32)
        tbl_15 = 0.05 * jax.random.normal(jax.random.fold_in(_tk, 500 + 15), (1000, 32), jnp.float32)
        tbl_16 = 0.05 * jax.random.normal(jax.random.fold_in(_tk, 500 + 16), (1250, 32), jnp.float32)
        tbl_17 = 0.05 * jax.random.normal(jax.random.fold_in(_tk, 500 + 17), (1250, 32), jnp.float32)
        tbl_18 = 0.05 * jax.random.normal(jax.random.fold_in(_tk, 500 + 18), (125000, 32), jnp.float32)
        tbl_19 = 0.05 * jax.random.normal(jax.random.fold_in(_tk, 500 + 19), (125000, 32), jnp.float32)
        tbl_20 = 0.05 * jax.random.normal(jax.random.fold_in(_tk, 500 + 20), (12500, 32), jnp.float32)
        tbl_21 = 0.05 * jax.random.normal(jax.random.fold_in(_tk, 500 + 21), (1000, 32), jnp.float32)
        tbl_22 = 0.05 * jax.random.normal(jax.random.fold_in(_tk, 500 + 22), (1000, 32), jnp.float32)
        tbl_23 = 0.05 * jax.random.normal(jax.random.fold_in(_tk, 500 + 23), (1250, 32), jnp.float32)
        tbl_24 = 0.05 * jax.random.normal(jax.random.fold_in(_tk, 500 + 24), (12500, 32), jnp.float32)
        tbl_25 = 0.05 * jax.random.normal(jax.random.fold_in(_tk, 500 + 25), (12500, 32), jnp.float32)
        tbl_26 = 0.05 * jax.random.normal(jax.random.fold_in(_tk, 500 + 26), (12500, 32), jnp.float32)
        tbl_27 = 0.05 * jax.random.normal(jax.random.fold_in(_tk, 500 + 27), (1250, 32), jnp.float32)
        tbl_28 = 0.05 * jax.random.normal(jax.random.fold_in(_tk, 500 + 28), (1250, 32), jnp.float32)
        tbl_29 = 0.05 * jax.random.normal(jax.random.fold_in(_tk, 500 + 29), (12500, 32), jnp.float32)
        tbl_30 = 0.05 * jax.random.normal(jax.random.fold_in(_tk, 500 + 30), (1250, 32), jnp.float32)
        tbl_31 = 0.05 * jax.random.normal(jax.random.fold_in(_tk, 500 + 31), (125000, 32), jnp.float32)
        tbl_32 = 0.05 * jax.random.normal(jax.random.fold_in(_tk, 500 + 32), (12500, 32), jnp.float32)
        tbl_33 = 0.05 * jax.random.normal(jax.random.fold_in(_tk, 500 + 33), (1250, 32), jnp.float32)
        tbl_34 = 0.05 * jax.random.normal(jax.random.fold_in(_tk, 500 + 34), (1250, 32), jnp.float32)
        tbl_35 = 0.05 * jax.random.normal(jax.random.fold_in(_tk, 500 + 35), (12500, 32), jnp.float32)
        tbl_36 = 0.05 * jax.random.normal(jax.random.fold_in(_tk, 500 + 36), (1000, 32), jnp.float32)
        tbl_37 = 0.05 * jax.random.normal(jax.random.fold_in(_tk, 500 + 37), (1000, 32), jnp.float32)
        tbl_38 = 0.05 * jax.random.normal(jax.random.fold_in(_tk, 500 + 38), (1250, 32), jnp.float32)
        _rk = jax.random.fold_in(_tk, 7)
        W_top1 = 0.0693375 * jax.random.normal(jax.random.fold_in(_tk, 801), (208, 512), jnp.float32)
        W_top2 = 0.0441942 * jax.random.normal(jax.random.fold_in(_tk, 802), (512, 256), jnp.float32)
        W_top3 = 0.0625 * jax.random.normal(jax.random.fold_in(_tk, 803), (256, 1), jnp.float32)
        b_top1 = jnp.zeros((512,), jnp.float32)
        b_top2 = jnp.zeros((256,), jnp.float32)
        return (dense_ctx, ids, tbl_0, tbl_1, tbl_2, tbl_3, tbl_4, tbl_5, tbl_6, tbl_7, tbl_8, tbl_9, tbl_10, tbl_11, tbl_12, tbl_13, tbl_14, tbl_15, tbl_16, tbl_17, tbl_18, tbl_19, tbl_20, tbl_21, tbl_22, tbl_23, tbl_24, tbl_25, tbl_26, tbl_27, tbl_28, tbl_29, tbl_30, tbl_31, tbl_32, tbl_33, tbl_34, tbl_35, tbl_36, tbl_37, tbl_38, W_top1, b_top1, W_top2, b_top2, W_top3)
    dense_ctx, ids, tbl_0, tbl_1, tbl_2, tbl_3, tbl_4, tbl_5, tbl_6, tbl_7, tbl_8, tbl_9, tbl_10, tbl_11, tbl_12, tbl_13, tbl_14, tbl_15, tbl_16, tbl_17, tbl_18, tbl_19, tbl_20, tbl_21, tbl_22, tbl_23, tbl_24, tbl_25, tbl_26, tbl_27, tbl_28, tbl_29, tbl_30, tbl_31, tbl_32, tbl_33, tbl_34, tbl_35, tbl_36, tbl_37, tbl_38, W_top1, b_top1, W_top2, b_top2, W_top3 = _rec_inputs()

    def _L0_rec_setup():
        import jax, jax.numpy as jnp
        import numpy as np
        LAYER_SIZES = (128, 128)

        def _cin_layer(h0, h, W):
            F0, Fi = (h0.shape[1], h.shape[1])
            K = W.shape[1]
            Wr = W.reshape(F0, Fi, K)
            return jnp.einsum('bid,bjd,ijk->bkd', h0, h, Wr)
        key = jax.random.key(seed)
        k1, k2, k3 = jax.random.split(key, 3)
        B, F0, D = (256, 39, 32)
        F1 = LAYER_SIZES[0] // 2
        x = jax.random.normal(k1, (B, F0, D), dtype=jnp.float32)
        W1 = jax.random.normal(k2, (F0 * F0, LAYER_SIZES[0]), dtype=jnp.float32) * 0.05
        W2 = jax.random.normal(k3, (F0 * F1, LAYER_SIZES[1]), dtype=jnp.float32) * 0.05
        return {'x': x, 'W1': W1, 'W2': W2}
    _L0_rec_all = _L0_rec_setup()
    _L0_rec_in = {k: v for k, v in _L0_rec_all.items() if k in ('W1', 'W2')}
    del _L0_rec_all
    return {'dense_ctx': dense_ctx, 'ids': ids, 'tbl_0': tbl_0, 'tbl_1': tbl_1, 'tbl_2': tbl_2, 'tbl_3': tbl_3, 'tbl_4': tbl_4, 'tbl_5': tbl_5, 'tbl_6': tbl_6, 'tbl_7': tbl_7, 'tbl_8': tbl_8, 'tbl_9': tbl_9, 'tbl_10': tbl_10, 'tbl_11': tbl_11, 'tbl_12': tbl_12, 'tbl_13': tbl_13, 'tbl_14': tbl_14, 'tbl_15': tbl_15, 'tbl_16': tbl_16, 'tbl_17': tbl_17, 'tbl_18': tbl_18, 'tbl_19': tbl_19, 'tbl_20': tbl_20, 'tbl_21': tbl_21, 'tbl_22': tbl_22, 'tbl_23': tbl_23, 'tbl_24': tbl_24, 'tbl_25': tbl_25, 'tbl_26': tbl_26, 'tbl_27': tbl_27, 'tbl_28': tbl_28, 'tbl_29': tbl_29, 'tbl_30': tbl_30, 'tbl_31': tbl_31, 'tbl_32': tbl_32, 'tbl_33': tbl_33, 'tbl_34': tbl_34, 'tbl_35': tbl_35, 'tbl_36': tbl_36, 'tbl_37': tbl_37, 'tbl_38': tbl_38, 'W_top1': W_top1, 'b_top1': b_top1, 'W_top2': W_top2, 'b_top2': b_top2, 'W_top3': W_top3, 'L0_rec_W1': _L0_rec_in['W1'], 'L0_rec_W2': _L0_rec_in['W2']}

def reference(dense_ctx, ids, tbl_0, tbl_1, tbl_2, tbl_3, tbl_4, tbl_5, tbl_6, tbl_7, tbl_8, tbl_9, tbl_10, tbl_11, tbl_12, tbl_13, tbl_14, tbl_15, tbl_16, tbl_17, tbl_18, tbl_19, tbl_20, tbl_21, tbl_22, tbl_23, tbl_24, tbl_25, tbl_26, tbl_27, tbl_28, tbl_29, tbl_30, tbl_31, tbl_32, tbl_33, tbl_34, tbl_35, tbl_36, tbl_37, tbl_38, W_top1, b_top1, W_top2, b_top2, W_top3, L0_rec_W1, L0_rec_W2):
    import jax
    import jax.numpy as jnp

    def _L0_rec_ref(x, W1, W2):
        import jax, jax.numpy as jnp
        import numpy as np
        LAYER_SIZES = (128, 128)

        def _cin_layer(h0, h, W):
            F0, Fi = (h0.shape[1], h.shape[1])
            K = W.shape[1]
            Wr = W.reshape(F0, Fi, K)
            return jnp.einsum('bid,bjd,ijk->bkd', h0, h, Wr)
        conv1 = _cin_layer(x, x, W1)
        half = LAYER_SIZES[0] // 2
        hidden1 = conv1[:, :half, :]
        final1 = conv1[:, half:, :]
        conv2 = _cin_layer(x, hidden1, W2)
        final = jnp.concatenate([final1, conv2], axis=1)
        return jnp.sum(final, axis=2)
    e = jnp.stack([tbl_0[ids[:, 0]], tbl_1[ids[:, 1]], tbl_2[ids[:, 2]], tbl_3[ids[:, 3]], tbl_4[ids[:, 4]], tbl_5[ids[:, 5]], tbl_6[ids[:, 6]], tbl_7[ids[:, 7]], tbl_8[ids[:, 8]], tbl_9[ids[:, 9]], tbl_10[ids[:, 10]], tbl_11[ids[:, 11]], tbl_12[ids[:, 12]], tbl_13[ids[:, 13]], tbl_14[ids[:, 14]], tbl_15[ids[:, 15]], tbl_16[ids[:, 16]], tbl_17[ids[:, 17]], tbl_18[ids[:, 18]], tbl_19[ids[:, 19]], tbl_20[ids[:, 20]], tbl_21[ids[:, 21]], tbl_22[ids[:, 22]], tbl_23[ids[:, 23]], tbl_24[ids[:, 24]], tbl_25[ids[:, 25]], tbl_26[ids[:, 26]], tbl_27[ids[:, 27]], tbl_28[ids[:, 28]], tbl_29[ids[:, 29]], tbl_30[ids[:, 30]], tbl_31[ids[:, 31]], tbl_32[ids[:, 32]], tbl_33[ids[:, 33]], tbl_34[ids[:, 34]], tbl_35[ids[:, 35]], tbl_36[ids[:, 36]], tbl_37[ids[:, 37]], tbl_38[ids[:, 38]]], axis=1)
    z = _L0_rec_ref(e, L0_rec_W1, L0_rec_W2)
    z = z.reshape(z.shape[0], -1)
    h = jnp.concatenate([z, dense_ctx], axis=1)
    h = jnp.maximum(h @ W_top1 + b_top1, 0.0)
    h = jnp.maximum(h @ W_top2 + b_top2, 0.0)
    y = h @ W_top3
    return y

_drawn_inputs = setup_inputs


def setup_inputs(seed=0):
    import zlib

    import numpy as np

    out = dict(_drawn_inputs(seed))
    spreads = {'b_top1': (0.0, 0.1), 'b_top2': (0.0, 0.1)}
    factors = {'tbl_0': 4.905,
     'tbl_1': 4.732,
     'tbl_2': 4.813,
     'tbl_3': 4.895,
     'tbl_4': 4.904,
     'tbl_5': 4.576,
     'tbl_6': 4.772,
     'tbl_7': 4.643,
     'tbl_8': 4.739,
     'tbl_9': 4.788,
     'tbl_10': 5.009,
     'tbl_11': 4.558,
     'tbl_12': 4.825,
     'tbl_13': 4.652,
     'tbl_14': 4.351,
     'tbl_15': 4.97,
     'tbl_16': 4.579,
     'tbl_17': 4.671,
     'tbl_18': 4.933,
     'tbl_19': 5.077,
     'tbl_20': 4.946,
     'tbl_21': 4.907,
     'tbl_22': 4.789,
     'tbl_23': 5.068,
     'tbl_24': 4.375,
     'tbl_25': 4.741,
     'tbl_26': 4.801,
     'tbl_27': 4.497,
     'tbl_28': 4.911,
     'tbl_29': 4.67,
     'tbl_30': 4.33,
     'tbl_31': 4.583,
     'tbl_32': 4.905,
     'tbl_33': 4.392,
     'tbl_34': 4.878,
     'tbl_35': 4.853,
     'tbl_36': 5.121,
     'tbl_37': 4.575,
     'tbl_38': 4.634,
     'L0_rec_W2': 5.796}
    for name, (base, spread) in spreads.items():
        noise = np.random.default_rng([zlib.crc32(name.encode()), seed]).standard_normal(out[name].shape)
        drawn = base * np.exp(spread * noise) if base else spread * noise
        out[name] = jnp.asarray(drawn.astype(out[name].dtype))
    for name, factor in factors.items():
        out[name] = (out[name] * factor).astype(out[name].dtype)
    return out
```

```python
def build(nc, dense_ctx, ids, tables, w1a, w1b, select, ident, w1, w2, wt1, bt1, wt2, bt2, wt3, out):
    from contextlib import ExitStack

    import concourse.bass as bass
    from concourse import mybir

    FP32 = mybir.dt.float32
    BF16 = mybir.dt.bfloat16
    I32 = mybir.dt.int32
    ALU = mybir.AluOpType
    ACT = mybir.ActivationFunctionType

    BATCH, F = ids.shape
    D = tables[0].shape[1]
    NCTX = dense_ctx.shape[1]
    K1 = w1.shape[1]
    HID = K1 // 2
    FIN1 = K1 - HID
    K2 = w2.shape[1]
    M1, M2 = wt2.shape
    ROWS = select.shape[0]
    NP = w1a.shape[1]
    P = 128
    G4 = P // D
    TB = P
    NTB = BATCH // TB
    TILES = TB // G4
    BLK = 8
    QB = TILES // BLK
    HALF = 512
    TH = HALF // P
    NH = BATCH // HALF
    TPH = NTB // NH
    ILO = (F + 1) // 2
    IHI = F - ILO
    HXW = HID + F
    GHI = HID
    FILLS = [(0, 3), (3, 6), (6, 8)]
    NF = len(FILLS)
    NZ = 2 * NP
    NG = 4
    MC1, MC2 = M1 // P, M2 // P
    NM = 2 + MC1 + MC2 + 1
    Z_FREE, MAIN_FREE, A_FREE, PG_FREE = 4, NG, 2, 2 + NF

    with ExitStack() as ctx:
        def sb(name, shape, dt=FP32):
            return ctx.enter_context(nc.sbuf_tensor(name, shape, dt))

        def pb(name):
            return ctx.enter_context(nc.psum_tensor(name, [P, 512], FP32))

        def sem(name):
            return ctx.enter_context(nc.semaphore(name))

        ids_sb = sb("ids_sb", [P, NTB, F], I32)
        idx = sb("idx", [P, F], I32)
        ident_f = sb("ident_f", [P, P])
        ident_b = sb("ident_b", [P, P], BF16)
        sel = sb("sel", [ROWS, 5 * ROWS], BF16)
        w1s = sb("w1s", [ROWS, NP, HID])
        w2f = sb("w2f", [P, ILO, K2])
        w1f = sb("w1f", [HXW, ILO, FIN1])
        wt1c = sb("wt1c", [K2, M1])
        wt1f = sb("wt1f", [FIN1 + NCTX, M1])
        wt2_sb = sb("wt2_sb", [P, MC1, M2])
        wt3_sb = sb("wt3_sb", [P, MC2])
        bt1_sb = sb("bt1_sb", [P, MC1])
        bt2_sb = sb("bt2_sb", [P, MC2])
        ctx_sb = sb("ctx_sb", [P, NTB, NCTX])
        gath = sb("gath", [P, F, D])
        xT = sb("xT", [P, F, TILES])
        resid = sb("resid", [P, BLK, F])
        parts = sb("parts", [P, 2, BLK, ROWS], BF16)
        xs = sb("xs", [ROWS, 2, 2 * HALF], BF16)
        hx = sb("hx", [P, QB, BLK, HXW])
        xblk = sb("xblk", [P, QB, BLK, G4, F])
        opA = sb("opA", [ROWS, 2, 2, 2, HALF])
        z = sb("z", [ROWS, 2 + 8, HALF])
        h_sb = sb("h_sb", [P, HALF])
        pq = sb("pq", [P, ILO, HALF])
        gq = sb("gq", [HXW, ILO, HALF])
        ctxT = sb("ctxT", [FIN1 + NCTX, BATCH])
        y_sb = sb("y_sb", [1, BATCH])
        w1a_sb = pq[0:ROWS, 8, 0:NP * HID].rearrange("p (n k) -> p n k", n=NP)
        w1b_sb = pq[0:ROWS, 9, 0:NP * HID].rearrange("p (n k) -> p n k", n=NP)
        sel_f = pq[0:ROWS, 10:12, :].rearrange("p a n -> p (a n)")[:, 0:5 * ROWS]
        r1 = pq[:, 0:MC1, :]
        r2 = pq[:, MC1:MC1 + MC2, :]
        c2_sb = pq[0:K2, MC1 + MC2, :]
        f1_sb = pq[0:FIN1 + NCTX, MC1 + MC2 + 1, :]

        bank_T = pb("bank_T")
        bank_A = [pb("bank_A0"), pb("bank_A1")]
        bank_B = [pb("bank_B0"), pb("bank_B1")]
        bank_H = pb("bank_H")
        bank_G = [pb("bank_G0"), pb("bank_G1")]
        partsT_ps = bank_T[:, :].bitcast(BF16)

        s_ids = sem("s_ids")
        s_sel = sem("s_sel")
        s_ident = sem("s_ident")
        s_w1 = sem("s_w1")
        s_ctx = sem("s_ctx")
        s_wfin = sem("s_wfin")
        s_wmlp = sem("s_wmlp")
        s_gath = sem("s_gath")
        s_out = sem("s_out")
        s_const = sem("s_const")
        s_clear = sem("s_clear")
        s_xT = sem("s_xT")
        s_resid = sem("s_resid")
        s_low = sem("s_low")
        s_z = sem("s_z")
        s_idx = sem("s_idx")
        s_issue = sem("s_issue")
        s_high = sem("s_high")
        s_mid = sem("s_mid")
        s_xcopy = sem("s_xcopy")
        s_xs = sem("s_xs")
        s_opA = sem("s_opA")
        s_h = sem("s_h")
        s_hT = sem("s_hT")
        s_pgc = sem("s_pgc")
        s_ctxT = sem("s_ctxT")
        s_fc = sem("s_fc")
        s_ctxps = sem("s_ctxps")
        s_partsT = sem("s_partsT")
        s_A = sem("s_A")
        s_B = sem("s_B")
        s_main = sem("s_main")
        s_ht = sem("s_ht")
        s_pg = sem("s_pg")
        s_fin = sem("s_fin")

        block = ctx.enter_context(nc.Block())

        @block.sync
        def _(sp):
            sp.dma_start(ids_sb[:, :, :], ids.rearrange("(t p) f -> p t f", p=P)).then_inc(s_ids, 16)
            sp.dma_start(ident_f[:, :], ident).then_inc(s_ident, 16)
            sp.dma_start(sel_f[:, :], select).then_inc(s_sel, 16)
            sp.dma_start(w1a_sb[:, :, :], w1a).then_inc(s_w1, 16)
            sp.dma_start(w1b_sb[:, :, :], w1b).then_inc(s_w1, 16)
            sp.dma_start(ctx_sb[:, :, :], dense_ctx.rearrange("(t p) c -> p t c", p=P)).then_inc(s_ctx, 16)
            w2v = w2.rearrange("(i j) m -> j i m", j=HID)
            sp.wait_ge(s_clear, 1)
            sp.dma_start(w2f[0:HID, :, :], w2v[:, 0:ILO, :]).then_inc(s_wfin, 16)
            sp.dma_start(w2f[HID:P, 0:IHI, :], w2v[:, ILO:F, :]).then_inc(s_wfin, 16)
            w1v = w1.rearrange("(c i) k -> c i k", i=F)
            sp.dma_start(w1f[0:F, :, :], w1v[:, 0:ILO, HID:K1]).then_inc(s_wfin, 16)
            sp.dma_start(w1f[GHI:HXW, 0:IHI, :], w1v[:, ILO:F, HID:K1]).then_inc(s_wfin, 16)
            sp.dma_start(wt1c[:, :], wt1[FIN1:FIN1 + K2, :]).then_inc(s_wmlp, 16)
            sp.dma_start(wt1f[0:FIN1, :], wt1[0:FIN1, :]).then_inc(s_wmlp, 16)
            sp.dma_start(wt1f[FIN1:, :], wt1[FIN1 + K2:, :]).then_inc(s_wmlp, 16)
            sp.dma_start(wt2_sb[:, :, :], wt2.rearrange("(c p) m -> p c m", p=P)).then_inc(s_wmlp, 16)
            with nc.allow_non_contiguous_dma("three small vectors"):
                sp.dma_start(wt3_sb[:, :], wt3.rearrange("(c p) o -> p (c o)", p=P)).then_inc(s_wmlp, 16)
                sp.dma_start(bt1_sb[:, :], bt1.rearrange("(c p) -> p c", p=P)).then_inc(s_wmlp, 16)
                sp.dma_start(bt2_sb[:, :], bt2.rearrange("(c p) -> p c", p=P)).then_inc(s_wmlp, 16)
            sp.wait_ge(s_fc, NM * (NH + 1))
            sp.dma_start(out.rearrange("b o -> o b"), y_sb[:, :]).then_inc(s_out, 16)
            sp.wait_ge(s_out, 16)

        @block.gpsimd
        def _(pool):
            pool.wait_ge(s_ids, 16)
            with pool.Fori(0, NTB) as t:
                with pool.If(t > 0):
                    pool.wait_ge(s_xT, t)
                nc.gpsimd.tensor_copy(idx[:, :], ids_sb[:, bass.ds(t, 1), :].rearrange("p a f -> p (a f)")).then_inc(s_idx, 1)
                pool.wait_ge(s_idx, t + 1)
                pool.sem_inc(s_issue, 1)
                for f in range(F):
                    pool.indirect_dma_start(
                        out=gath[:, f, :], out_offset=None, in_=tables[f],
                        in_offset=bass.IndirectOffsetOnAxis(ap=idx[:, f:f + 1], axis=0)).then_inc(s_gath, 16)

        def x_tiles(q):
            return xT[:, :, q * BLK:(q + 1) * BLK].rearrange("p f t -> p t f")

        def part(q, n):
            return parts[:, q % 2, :, n * F:(n + 1) * F]

        @block.vector
        def _(dve):
            dve.wait_ge(s_ident, 16)
            nc.vector.tensor_copy(ident_b[:, :], ident_f[:, :])
            dve.wait_ge(s_sel, 16)
            nc.vector.tensor_copy(sel[:, :], sel_f[:, :])
            dve.wait_ge(s_w1, 32)
            nc.vector.tensor_tensor(w1s[:, :, :], w1a_sb[:, :, :], w1b_sb[:, :, :], ALU.add).then_inc(s_const, 1)
            nc.vector.memset(xblk[:, :, :, :, :], 0.0)
            nc.vector.memset(gq[0:GHI, :, :], 0.0)
            nc.vector.memset(w1f[:, :, :], 0.0)
            nc.vector.memset(gq[GHI:HXW, IHI:ILO, :], 0.0)
            nc.vector.memset(w2f[HID:P, IHI:ILO, :], 0.0)
            nc.vector.memset(pq[HID:P, IHI:ILO, :], 0.0).then_inc(s_clear, 1)

            def transpose_tile(t):
                dve.wait_ge(s_gath, (t + 1) * (16 * F))
                nc.vector.transpose(xT[:, :, :].rearrange("p f t -> p (f t)"),
                                    gath[:, :, :].rearrange("p f d -> p (f d)")).then_inc(s_xT, 1)

            def residual(k, q):
                dve.wait_ge(s_high, k + 1)
                if not (isinstance(k, int) and k == 0):
                    dve.wait_ge(s_low, k)
                nc.vector.tensor_tensor(resid[:, :, :], x_tiles(q), part(q, 0), ALU.subtract).then_inc(s_resid, 1)

            def low_part(k, q):
                dve.wait_ge(s_mid, k + 1)
                nc.vector.tensor_tensor(part(q, 2), resid[:, :, :], part(q, 1), ALU.subtract).then_inc(s_low, 1)

            def products(k, q, group):
                a = opA[:, q % 2, :, :, :]
                dve.wait_ge(s_main, NG * k + {0: 1, 1: 4, 2: 3, 3: 6}[group])
                for h in range(2):
                    if group == 0:
                        dve.wait_ge(s_opA, 4 * k + A_FREE + 3 + h)
                        nc.vector.tensor_tensor(z[:, h, :], a[:, 0, h, :], a[:, 1, h, :], ALU.mult).then_inc(s_z, 1)
                    else:
                        v = group - 1
                        dve.wait_ge(s_B, 6 * k + 2 * v + h + 1)
                        for u in range(2):
                            nc.vector.tensor_tensor(z[:, 2 + 4 * (v % 2) + 2 * h + u, :], a[:, u, h, :],
                                                    bank_B[h][0:ROWS, :], ALU.mult).then_inc(s_z, 1)

            transpose_tile(0)
            for q in range(2):
                residual(q, q)
                low_part(q, q)
            with dve.Fori(0, NTB) as t:
                for q in range(QB):
                    k = t * QB + q
                    qn = (q + 2) % QB
                    products(k, q, 0)
                    products(k, q, 1)
                    if q < 2:
                        residual(k + 2, qn)
                    elif q == 2:
                        with dve.If(t < NTB - 1):
                            transpose_tile(t + 1)
                            residual(k + 2, qn)
                    else:
                        with dve.If(t < NTB - 1):
                            residual(k + 2, qn)
                    products(k, q, 2)
                    if q < 2:
                        low_part(k + 2, qn)
                    else:
                        with dve.If(t < NTB - 1):
                            low_part(k + 2, qn)
                    products(k, q, 3)

        @block.scalar
        def _(act):
            act.sem_inc(s_opA, A_FREE)
            act.sem_inc(s_h, 1)
            act.sem_inc(s_hT, 1)
            act.sem_inc(s_pgc, PG_FREE)
            act.sem_inc(s_fc, NM)

            def copy(dst, src):
                return nc.scalar.activation(dst, src, ACT.Copy)

            def high_part(q):
                copy(part(q, 0), x_tiles(q)).then_inc(s_high, 1)

            def mid_part(k, q):
                act.wait_ge(s_resid, k + 1)
                copy(part(q, 1), resid[:, :, :]).then_inc(s_mid, 1)

            def place_x(q):
                copy(hx[:, q, :, HID:HXW], x_tiles(q))
                for g in range(G4):
                    rows = slice(g * D, (g + 1) * D)
                    last = copy(xblk[rows, q, :, g, :], x_tiles(q)[rows])
                last.then_inc(s_xcopy, 1)

            def copy_parts(k, q):
                act.wait_ge(s_partsT, k + 1)
                copy(xs[:, q % 2, :], partsT_ps[0:ROWS, :]).then_inc(s_xs, 1)

            def copy_A(k, q):
                act.wait_ge(s_z, NZ * (k - 1) + Z_FREE)
                for u in range(2):
                    for h in range(2):
                        act.wait_ge(s_A, 4 * k + 2 * u + h + 1)
                        copy(opA[:, q % 2, u, h, :], bank_A[h][0:ROWS, :]).then_inc(s_opA, 1)

            def copy_hidden(k):
                act.wait_ge(s_main, NG * (k + 1) + MAIN_FREE)
                act.wait_ge(s_ht, k + 1)
                copy(h_sb[:, :], bank_H[:, :]).then_inc(s_h, 1)

            def copy_hiddenT(k, q):
                act.wait_ge(s_ht, k + 2)
                copy(hx[:, q, :, 0:HID].rearrange("p (g t) c -> p t g c", g=2),
                     bank_T[:, :].rearrange("p (t g c) -> p t g c", t=TH, g=2)).then_inc(s_hT, 1)

            def copy_pg(k, q, i):
                for j, (t0, t1) in enumerate(FILLS):
                    act.wait_ge(s_pg, NF * (k + 1) + j + 1)
                    src = bank_G[j % 2][:, 0:(t1 - t0) * G4 * F].rearrange("p (t g f) -> p f g t", g=G4, f=F)
                    def col(dst):
                        view = dst.rearrange("p f (i g t) -> p f i g t", i=TPH, g=G4)
                        view = view[:, :, bass.ds(i, 1), :, q * BLK + t0:q * BLK + t1]
                        return view.rearrange("p f i g t -> p f (i g) t")
                    copy(col(pq[0:HID, :, :]), src[0:HID, 0:ILO])
                    copy(col(pq[HID:P, 0:IHI, :]), src[0:HID, ILO:F])
                    copy(col(gq[0:F, :, :]), src[HID:HXW, 0:ILO])
                    copy(col(gq[GHI:HXW, 0:IHI, :]), src[HID:HXW, ILO:F]).then_inc(s_pgc, 1)

            for n in range(2):
                act.wait_ge(s_ctxps, n + 1)
                copy(ctxT[FIN1:, n * 512:(n + 1) * 512], bank_G[n][0:NCTX, :]).then_inc(s_ctxT, 1)
            act.wait_ge(s_xT, 1)
            high_part(0)
            mid_part(0, 0)
            high_part(1)
            mid_part(1, 1)
            copy_parts(0, 0)
            for u in range(2):
                for h in range(2):
                    act.wait_ge(s_A, 2 * u + h + 1)
                    copy(opA[:, 0, u, h, :], bank_A[h][0:ROWS, :]).then_inc(s_opA, 1)
            act.wait_ge(s_clear, 1)
            place_x(0)
            place_x(1)
            with act.Fori(0, NH) as hb:
                with act.Fori(0, TPH) as i:
                    t = hb * TPH + i
                    for q in range(QB):
                        k = t * QB + q
                        qp, qn, q2 = (q - 1) % QB, (q + 1) % QB, (q + 2) % QB

                        def split_ahead():
                            act.wait_ge(s_partsT, k + 1)
                            high_part(q2)

                        def before():
                            copy_hidden(k - 1)

                        def ahead_x():
                            place_x(q2)
                            mid_part(k + 2, q2)

                        if q > 0:
                            copy_hidden(k - 1)
                        else:
                            with act.If(i > 0):
                                copy_hidden(k - 1)
                        if q < 2:
                            split_ahead()
                        else:
                            with act.If(t < NTB - 1):
                                if q == 2:
                                    act.wait_ge(s_xT, t + 2)
                                split_ahead()
                        if q > 0:
                            copy_hiddenT(k - 1, qp)
                        else:
                            with act.If(i > 0):
                                copy_hiddenT(k - 1, qp)
                        if q < 2:
                            ahead_x()
                        else:
                            with act.If(t < NTB - 1):
                                ahead_x()
                        if q > 0:
                            copy_pg(k - 1, qp, i)
                        else:
                            with act.If(i > 0):
                                copy_pg(k - 1, qp, nc.s_assert_within(
                                    i - 1, 0, TPH - 1, skip_runtime_bounds_check_because="the branch is taken for i > 0"))
                        if q < QB - 1:
                            copy_parts(k + 1, qn)
                            copy_A(k + 1, qn)
                        else:
                            with act.If(t < NTB - 1):
                                copy_parts(k + 1, qn)
                                copy_A(k + 1, qn)
                last = (hb + 1) * (TPH * QB) - 1
                copy_hidden(last)
                copy_hiddenT(last, QB - 1)
                copy_pg(last, QB - 1, TPH - 1)

                done = hb * NM

                def fin(n):
                    act.wait_ge(s_fin, done + n + 1)
                    return bank_G[n % 2]
                copy(c2_sb[:, :], fin(0)[0:K2, :]).then_inc(s_fc, 1)
                act.wait_ge(s_ctxT, 2)
                copy(f1_sb[FIN1:, :], ctxT[FIN1:, bass.ds(hb * HALF, HALF)])
                b1 = fin(1)
                copy(f1_sb[0:FIN1, 0:HALF // 2], b1[0:FIN1, 0:HALF // 2])
                copy(f1_sb[0:FIN1, HALF // 2:HALF], b1[64:64 + FIN1, 0:HALF // 2]).then_inc(s_fc, 1)
                act.wait_ge(s_wmlp, 16 * 7)
                for c in range(MC1):
                    nc.scalar.activation(r1[:, c, :], fin(2 + c)[:, :], ACT.Relu, bias=bt1_sb[:, c:c + 1]).then_inc(s_fc, 1)
                for c in range(MC2):
                    nc.scalar.activation(r2[:, c, :], fin(2 + MC1 + c)[:, :], ACT.Relu, bias=bt2_sb[:, c:c + 1]).then_inc(s_fc, 1)
                copy(y_sb[:, bass.ds(hb * HALF, HALF)], fin(NM - 1)[0:1, :]).then_inc(s_fc, 1)

        @block.tensor
        def _(pe):
            pe.sem_inc(s_main, MAIN_FREE)
            pe.sem_inc(s_ht, 1)
            pe.sem_inc(s_pg, NF)
            pe.sem_inc(s_z, Z_FREE)

            def matmul(dst, lhsT, rhs, first=True, last=True):
                return nc.tensor.matmul(dst, lhsT, rhs, start=first, stop=last)

            def transpose_parts(k, q):
                pe.wait_ge(s_low, k + 1)
                pe.wait_ge(s_hT, k)
                for t in range(BLK):
                    last = nc.tensor.transpose(partsT_ps[0:ROWS, t * P:(t + 1) * P], parts[:, q % 2, t, :], ident_b[:, :])
                last.then_inc(s_partsT, 1)

            def operand(n, q, h, bank, signal):
                matmul(bank[h][0:ROWS, :], sel[:, n * ROWS:(n + 1) * ROWS],
                       xs[:, q % 2, h * HALF:(h + 1) * HALF]).then_inc(signal, 1)

            def operand_A(k, q, u):
                if u == 0:
                    pe.wait_ge(s_xs, k + 1)
                for h in range(2):
                    pe.wait_ge(s_opA, 4 * k + 2 * u + h + 1)
                    operand(u, q, h, bank_A, s_A)

            def operand_B(k, q, v, h):
                pe.wait_ge(s_z, NZ * k + Z_FREE + (-2 + 2 * h if v == 0 else 4 * v + 2 * h))
                operand(2 + v, q, h, bank_B, s_B)

            def main(k, group):
                if group == 0:
                    pe.wait_ge(s_h, k + 1)
                pe.wait_ge(s_z, NZ * k + Z_FREE + 2 + 4 * group)
                room = 2 + 4 * ((group - 1) % 2)
                slots = [(0, 0, 1)] if group == 0 else [(2 * group - 1 + u, room + u, room + 2 + u) for u in range(2)]
                for prod, *zs in slots:
                    for h in range(2):
                        last = matmul(bank_H[64 * h:64 * h + HID, :], w1s[:, prod, :], z[:, zs[h], :],
                                      first=prod == 0, last=prod == NP - 1)
                last.then_inc(s_main, 1)

            def transpose_hidden(k):
                pe.wait_ge(s_h, k + 2)
                with_t = k + 1
                pe.wait_ge(s_xs, with_t + 1)
                for t in range(TH):
                    last = nc.tensor.transpose(bank_T[:, t * P:(t + 1) * P], h_sb[:, t * P:(t + 1) * P], ident_f[:, :])
                last.then_inc(s_ht, 1)

            def fill_pg(k, q, j):
                if j == 0:
                    pe.wait_ge(s_hT, k + 2)
                    pe.wait_ge(s_xcopy, k + 1)
                pe.wait_ge(s_pgc, NF * k + j - 1 + PG_FREE)
                for n, t in enumerate(range(*FILLS[j])):
                    last = matmul(bank_G[j % 2][0:HXW, n * G4 * F:(n + 1) * G4 * F], hx[:, q, t, :],
                                  xblk[:, q, t, :, :].rearrange("p g f -> p (g f)"))
                last.then_inc(s_pg, 1)

            pe.wait_ge(s_ident, 16)
            pe.wait_ge(s_ctx, 16)
            for n in range(2):
                for t in range(NTB // 2):
                    last = nc.tensor.transpose(bank_G[n][0:NCTX, t * P:(t + 1) * P], ctx_sb[:, n * NTB // 2 + t, :], ident_f[:, :])
                last.then_inc(s_ctxps, 1)
            pe.wait_ge(s_const, 1)
            pe.wait_ge(s_ctxT, 2)
            pe.wait_ge(s_low, 1)
            for t in range(BLK):
                last = nc.tensor.transpose(partsT_ps[0:ROWS, t * P:(t + 1) * P], parts[:, 0, t, :], ident_b[:, :])
            last.then_inc(s_partsT, 1)
            operand_A(0, 0, 0)
            operand_A(0, 0, 1)
            with pe.Fori(0, NH) as hb:
                with pe.Fori(0, TPH) as i:
                    t = hb * TPH + i
                    for q in range(QB):
                        k = t * QB + q
                        qp, qn = (q - 1) % QB, (q + 1) % QB

                        def earlier(step, arg=None):
                            def run():
                                if arg is None:
                                    transpose_hidden(k - 1)
                                else:
                                    fill_pg(k - 1, qp, arg)
                            if q > 0:
                                run()
                            else:
                                with pe.If(i > 0):
                                    run()
                        operand_B(k, q, 0, 0)
                        operand_B(k, q, 0, 1)
                        earlier("hidden")
                        main(k, 0)
                        operand_B(k, q, 1, 0)
                        earlier("fill", 0)
                        operand_B(k, q, 1, 1)
                        main(k, 1)
                        operand_B(k, q, 2, 0)
                        earlier("fill", 1)
                        operand_B(k, q, 2, 1)
                        if q < QB - 1:
                            transpose_parts(k + 1, qn)
                        else:
                            with pe.If(t < NTB - 1):
                                transpose_parts(k + 1, qn)
                        main(k, 2)
                        earlier("fill", 2)
                        if q < QB - 1:
                            operand_A(k + 1, qn, 0)
                            operand_A(k + 1, qn, 1)
                        else:
                            with pe.If(t < NTB - 1):
                                operand_A(k + 1, qn, 0)
                                operand_A(k + 1, qn, 1)
                        main(k, 3)
                last_k = (hb + 1) * (TPH * QB) - 1
                pe.wait_ge(s_h, last_k + 2)
                with pe.If(hb < NH - 1):
                    pe.wait_ge(s_xs, last_k + 2)
                for t in range(TH):
                    last = nc.tensor.transpose(bank_T[:, t * P:(t + 1) * P], h_sb[:, t * P:(t + 1) * P], ident_f[:, :])
                last.then_inc(s_ht, 1)
                for j in range(NF):
                    fill_pg(last_k, QB - 1, j)

                done = hb * NM
                pe.wait_ge(s_wfin, 16 * 4)
                pe.wait_ge(s_wmlp, 16 * 7)
                pe.wait_ge(s_pgc, NF * (last_k + 1) + PG_FREE)
                for f in range(ILO):
                    last = matmul(bank_G[0][:, :], w2f[:, f, :], pq[:, f, :], f == 0, f == ILO - 1)
                last.then_inc(s_fin, 1)
                for f in range(ILO):
                    for h in range(2):
                        last = matmul(bank_G[1][64 * h:64 * h + FIN1, 0:HALF // 2], w1f[:, f, :],
                                      gq[:, f, h * HALF // 2:(h + 1) * HALF // 2], f == 0, f == ILO - 1)
                last.then_inc(s_fin, 1)
                for c in range(MC1):
                    pe.wait_ge(s_fc, done + NM + max(2, 2 + c - 1))
                    cols = slice(c * P, (c + 1) * P)
                    matmul(bank_G[c % 2][:, :], wt1c[:, cols], c2_sb[:, :], True, False)
                    matmul(bank_G[c % 2][:, :], wt1f[:, cols], f1_sb[:, :], False, True).then_inc(s_fin, 1)
                for c in range(MC2):
                    pe.wait_ge(s_fc, done + NM + 2 + MC1)
                    for kc in range(MC1):
                        last = matmul(bank_G[c % 2][:, :], wt2_sb[:, kc, c * P:(c + 1) * P], r1[:, kc, :], kc == 0, kc == MC1 - 1)
                    last.then_inc(s_fin, 1)
                pe.wait_ge(s_fc, done + NM + NM - 1)
                for kc in range(MC2):
                    last = matmul(bank_G[0][0:1, :], wt3_sb[:, kc:kc + 1], r2[:, kc, :], kc == 0, kc == MC2 - 1)
                last.then_inc(s_fin, 1)
                pe.wait_ge(s_fc, done + NM + NM)


ROTATIONS = [(0, 0, 0), (19, 9, 29), (17, 0, 21), (4, 14, 28), (7, 3, 16)]
PRODUCTS = [(0, 1), (0, 2), (1, 2), (0, 3), (1, 3), (0, 4), (1, 4)]


def pair_rows(fields):
    seen, direct, swapped = set(), [], []
    for a, b in PRODUCTS:
        for ra, rb in zip(ROTATIONS[a], ROTATIONS[b]):
            distance = min((ra - rb) % fields, (rb - ra) % fields)
            new = distance not in seen
            seen.add(distance)
            for i in range(fields):
                p, q = (i + ra) % fields, (i + rb) % fields
                direct.append(p * fields + q if new else -1)
                swapped.append(q * fields + p if new and distance else -1)
    assert len(seen) == fields // 2 + 1
    return direct, swapped


def kernel(**inputs):
    import numpy as np
    import concourse.bacc as bacc
    from concourse import mybir
    from concourse.bass_utils import run_bass_kernel_spmd

    batch, fields = inputs["ids"].shape
    hidden = inputs["L0_rec_W1"].shape[1] // 2
    rows = 3 * fields

    w1 = np.asarray(inputs["L0_rec_W1"])
    padded = np.concatenate([w1[:, :hidden], np.zeros((1, hidden), w1.dtype)])
    w1a, w1b = (np.ascontiguousarray(padded[np.array(r)].reshape(len(PRODUCTS), rows, hidden).transpose(1, 0, 2))
                for r in pair_rows(fields))
    select = np.zeros((3, fields, 5, 3, fields), np.float32)
    for n, rots in enumerate(ROTATIONS):
        for r, off in enumerate(rots):
            for i in range(fields):
                select[:, (i + off) % fields, n, r, i] = 1.0

    arrays = {"dense_ctx": inputs["dense_ctx"], "ids": inputs["ids"]}
    arrays.update({f"tbl_{f}": inputs[f"tbl_{f}"] for f in range(fields)})
    arrays.update({"w1a": w1a, "w1b": w1b, "select": select.reshape(rows, 5 * rows), "ident": np.eye(128, dtype=np.float32),
                   "w1": w1, "w2": inputs["L0_rec_W2"], "wt1": inputs["W_top1"], "bt1": inputs["b_top1"],
                   "wt2": inputs["W_top2"], "bt2": inputs["b_top2"], "wt3": inputs["W_top3"]})
    nc = bacc.Bacc("TRN2", target_bir_lowering=False, num_devices=1)
    feeds, aps = {}, {}
    for name, a in arrays.items():
        a = np.ascontiguousarray(a)
        feeds[f"in_{name}"] = a
        aps[name] = nc.dram_tensor(f"in_{name}", a.shape, mybir.dt.from_np(a.dtype), kind="ExternalInput").ap()
    out = nc.dram_tensor("out_y", (batch, 1), mybir.dt.float32, kind="ExternalOutput").ap()
    build(nc, aps["dense_ctx"], aps["ids"], [aps[f"tbl_{f}"] for f in range(fields)], aps["w1a"], aps["w1b"],
          aps["select"], aps["ident"], aps["w1"], aps["w2"], aps["wt1"], aps["bt1"], aps["wt2"], aps["bt2"], aps["wt3"], out)
    result = run_bass_kernel_spmd(nc, [feeds], core_ids=[0])
    return result.results[0]["out_y"]
```

```python
def build(nc, dense_ctx, ids, tables, w1a, w1b, select, ident, w1, w2, wt1, bt1, wt2, bt2, wt3, out):
    from contextlib import ExitStack

    import concourse.bass as bass
    from concourse import mybir

    FP32 = mybir.dt.float32
    BF16 = mybir.dt.bfloat16
    I32 = mybir.dt.int32
    ALU = mybir.AluOpType
    ACT = mybir.ActivationFunctionType

    BATCH, F = ids.shape
    D = tables[0].shape[1]
    NCTX = dense_ctx.shape[1]
    K1 = w1.shape[1]
    HID = K1 // 2
    FIN1 = K1 - HID
    K2 = w2.shape[1]
    M1, M2 = wt2.shape
    ROWS = select.shape[0]
    NP = w1a.shape[1]
    P = 128
    G4 = P // D
    TB = P
    NTB = BATCH // TB
    TILES = TB // G4
    BLK = 8
    QB = TILES // BLK
    HALF = 512
    TH = HALF // P
    NH = BATCH // HALF
    TPH = NTB // NH
    ILO = (F + 1) // 2
    IHI = F - ILO
    HXW = HID + F
    GHI = HID
    FILLS = [(0, 3), (3, 6), (6, 8)]
    NF = len(FILLS)
    NZ = 2 * NP
    BY_B0, BY_B1, SELF, BY_B2 = range(4)
    NG = 4
    Z_OF = [0, 4, 8, 10]
    ROOM = [0, 4, 0, 8]
    ROOM_AFTER = [-1, -2, 1, 0]
    WEIGHTS = [(1, 2), (3, 4), (0,), (5, 6)]
    MC1, MC2 = M1 // P, M2 // P
    NM = 2 + MC1 + MC2 + 1
    Z_FREE, MAIN_FREE, A_FREE, PG_FREE = 4, NG, 2, 2 + 2 * NF

    with ExitStack() as ctx:
        def sb(name, shape, dt=FP32):
            return ctx.enter_context(nc.sbuf_tensor(name, shape, dt))

        def pb(name):
            return ctx.enter_context(nc.psum_tensor(name, [P, 512], FP32))

        def sem(name):
            return ctx.enter_context(nc.semaphore(name))

        ids_sb = sb("ids_sb", [P, NTB, F], I32)
        idx = sb("idx", [P, F], I32)
        ident_f = sb("ident_f", [P, P])
        ident_b = sb("ident_b", [P, P], BF16)
        sel = sb("sel", [ROWS, 5 * ROWS], BF16)
        w1s = sb("w1s", [ROWS, NP, HID])
        w2f = sb("w2f", [P, ILO, K2])
        w1f = sb("w1f", [HXW, ILO, FIN1])
        wt1c = sb("wt1c", [K2, M1])
        wt1f = sb("wt1f", [FIN1 + NCTX, M1])
        wt2_sb = sb("wt2_sb", [P, MC1, M2])
        wt3_sb = sb("wt3_sb", [P, MC2])
        bt1_sb = sb("bt1_sb", [P, MC1])
        bt2_sb = sb("bt2_sb", [P, MC2])
        ctx_sb = sb("ctx_sb", [P, NTB, NCTX])
        gath = sb("gath", [P, F, D])
        xT = sb("xT", [P, F, TILES])
        resid = sb("resid", [P, BLK, F])
        parts = sb("parts", [P, 2, BLK, ROWS], BF16)
        xs = sb("xs", [ROWS, 2, 2 * HALF], BF16)
        hx = sb("hx", [P, QB, BLK, HXW])
        xblk = sb("xblk", [P, QB, BLK, G4, F])
        opA = sb("opA", [ROWS, 2, 2, 2, HALF])
        z = sb("z", [ROWS, 3 * 4, HALF])
        h_sb = sb("h_sb", [P, HALF])
        pq = sb("pq", [P, ILO, HALF])
        gq = sb("gq", [HXW, ILO, HALF])
        rows_sb = sb("rows_sb", [FIN1 + NCTX, BATCH])
        ctxT = rows_sb[FIN1:, :]
        y_sb = rows_sb[0:1, :]
        w1a_sb = pq[0:ROWS, 8, 0:NP * HID].rearrange("p (n k) -> p n k", n=NP)
        w1b_sb = pq[0:ROWS, 9, 0:NP * HID].rearrange("p (n k) -> p n k", n=NP)
        sel_f = pq[0:ROWS, 10:12, :].rearrange("p a n -> p (a n)")[:, 0:5 * ROWS]
        r1 = pq[:, 0:MC1, :]
        r2 = pq[:, MC1:MC1 + MC2, :]
        c2_sb = pq[0:K2, MC1 + MC2, :]
        f1_sb = pq[0:FIN1 + NCTX, MC1 + MC2 + 1, :]

        bank_T = pb("bank_T")
        bank_A = [pb("bank_A0"), pb("bank_A1")]
        bank_B = [pb("bank_B0"), pb("bank_B1")]
        bank_H = pb("bank_H")
        bank_G = [pb("bank_G0"), pb("bank_G1")]
        partsT_ps = bank_T[:, :].bitcast(BF16)

        s_ids = sem("s_ids")
        s_sel = sem("s_sel")
        s_ident = sem("s_ident")
        s_w1 = sem("s_w1")
        s_ctx = sem("s_ctx")
        s_wfin = sem("s_wfin")
        s_wmlp = sem("s_wmlp")
        s_gath = sem("s_gath")
        s_out = sem("s_out")
        s_const = sem("s_const")
        s_clear = sem("s_clear")
        s_xT = sem("s_xT")
        s_resid = sem("s_resid")
        s_low = sem("s_low")
        s_z = sem("s_z")
        s_idx = sem("s_idx")
        s_issue = sem("s_issue")
        s_high = sem("s_high")
        s_mid = sem("s_mid")
        s_xcopy = sem("s_xcopy")
        s_xs = sem("s_xs")
        s_opA = sem("s_opA")
        s_h = sem("s_h")
        s_hT = sem("s_hT")
        s_pgc = sem("s_pgc")
        s_ctxT = sem("s_ctxT")
        s_fc = sem("s_fc")
        s_ctxps = sem("s_ctxps")
        s_partsT = sem("s_partsT")
        s_A = sem("s_A")
        s_B = sem("s_B")
        s_main = sem("s_main")
        s_ht = sem("s_ht")
        s_pg = sem("s_pg")
        s_fin = sem("s_fin")

        block = ctx.enter_context(nc.Block())

        @block.sync
        def _(sp):
            sp.dma_start(ids_sb[:, :, :], ids.rearrange("(t p) f -> p t f", p=P)).then_inc(s_ids, 16)
            sp.dma_start(ident_f[:, :], ident).then_inc(s_ident, 16)
            sp.dma_start(sel_f[:, :], select).then_inc(s_sel, 16)
            sp.dma_start(w1a_sb[:, :, :], w1a).then_inc(s_w1, 16)
            sp.dma_start(w1b_sb[:, :, :], w1b).then_inc(s_w1, 16)
            sp.dma_start(ctx_sb[:, :, :], dense_ctx.rearrange("(t p) c -> p t c", p=P)).then_inc(s_ctx, 16)
            w2v = w2.rearrange("(i j) m -> j i m", j=HID)
            sp.wait_ge(s_clear, 1)
            sp.dma_start(w2f[0:HID, :, :], w2v[:, 0:ILO, :]).then_inc(s_wfin, 16)
            sp.dma_start(w2f[HID:P, 0:IHI, :], w2v[:, ILO:F, :]).then_inc(s_wfin, 16)
            w1v = w1.rearrange("(c i) k -> c i k", i=F)
            sp.dma_start(w1f[0:F, :, :], w1v[:, 0:ILO, HID:K1]).then_inc(s_wfin, 16)
            sp.dma_start(w1f[GHI:HXW, 0:IHI, :], w1v[:, ILO:F, HID:K1]).then_inc(s_wfin, 16)
            sp.dma_start(wt1c[:, :], wt1[FIN1:FIN1 + K2, :]).then_inc(s_wmlp, 16)
            sp.dma_start(wt1f[0:FIN1, :], wt1[0:FIN1, :]).then_inc(s_wmlp, 16)
            sp.dma_start(wt1f[FIN1:, :], wt1[FIN1 + K2:, :]).then_inc(s_wmlp, 16)
            sp.dma_start(wt2_sb[:, :, :], wt2.rearrange("(c p) m -> p c m", p=P)).then_inc(s_wmlp, 16)
            with nc.allow_non_contiguous_dma("three small vectors"):
                sp.dma_start(wt3_sb[:, :], wt3.rearrange("(c p) o -> p (c o)", p=P)).then_inc(s_wmlp, 16)
                sp.dma_start(bt1_sb[:, :], bt1.rearrange("(c p) -> p c", p=P)).then_inc(s_wmlp, 16)
                sp.dma_start(bt2_sb[:, :], bt2.rearrange("(c p) -> p c", p=P)).then_inc(s_wmlp, 16)
            sp.wait_ge(s_fc, NM * (NH + 1))
            sp.dma_start(out.rearrange("b o -> o b"), y_sb[:, :]).then_inc(s_out, 16)
            sp.wait_ge(s_out, 16)

        @block.gpsimd
        def _(pool):
            pool.wait_ge(s_ids, 16)
            with pool.Fori(0, NTB) as t:
                with pool.If(t > 0):
                    pool.wait_ge(s_xT, t)
                nc.gpsimd.tensor_copy(idx[:, :], ids_sb[:, bass.ds(t, 1), :].rearrange("p a f -> p (a f)")).then_inc(s_idx, 1)
                pool.wait_ge(s_idx, t + 1)
                pool.sem_inc(s_issue, 1)
                for f in range(F):
                    pool.indirect_dma_start(
                        out=gath[:, f, :], out_offset=None, in_=tables[f],
                        in_offset=bass.IndirectOffsetOnAxis(ap=idx[:, f:f + 1], axis=0)).then_inc(s_gath, 16)

        def x_tiles(q):
            return xT[:, :, q * BLK:(q + 1) * BLK].rearrange("p f t -> p t f")

        def part(q, n):
            return parts[:, q % 2, :, n * F:(n + 1) * F]

        @block.vector
        def _(dve):
            dve.wait_ge(s_ident, 16)
            nc.vector.tensor_copy(ident_b[:, :], ident_f[:, :])
            dve.wait_ge(s_sel, 16)
            nc.vector.tensor_copy(sel[:, :], sel_f[:, :])
            dve.wait_ge(s_w1, 32)
            nc.vector.tensor_tensor(w1s[:, :, :], w1a_sb[:, :, :], w1b_sb[:, :, :], ALU.add).then_inc(s_const, 1)
            nc.vector.memset(xblk[:, :, :, :, :], 0.0)
            nc.vector.memset(gq[0:GHI, :, :], 0.0)
            nc.vector.memset(w1f[:, :, :], 0.0)
            nc.vector.memset(gq[GHI:HXW, IHI:ILO, :], 0.0)
            nc.vector.memset(w2f[HID:P, IHI:ILO, :], 0.0)
            nc.vector.memset(pq[HID:P, IHI:ILO, :], 0.0).then_inc(s_clear, 1)

            def transpose_tile(t):
                dve.wait_ge(s_gath, (t + 1) * (16 * F))
                nc.vector.transpose(xT[:, :, :].rearrange("p f t -> p (f t)"),
                                    gath[:, :, :].rearrange("p f d -> p (f d)")).then_inc(s_xT, 1)

            def residual(k, q):
                dve.wait_ge(s_high, k + 1)
                if not (isinstance(k, int) and k == 0):
                    dve.wait_ge(s_low, k)
                nc.vector.tensor_tensor(resid[:, :, :], x_tiles(q), part(q, 0), ALU.subtract).then_inc(s_resid, 1)

            def low_part(k, q):
                dve.wait_ge(s_mid, k + 1)
                nc.vector.tensor_tensor(part(q, 2), resid[:, :, :], part(q, 1), ALU.subtract).then_inc(s_low, 1)

            def products(k, q, group):
                a = opA[:, q % 2, :, :, :]
                dve.wait_ge(s_main, NG * k + ROOM_AFTER[group] + MAIN_FREE)
                for h in range(2):
                    if group == SELF:
                        nc.vector.tensor_tensor(z[:, ROOM[group] + h, :], a[:, 0, h, :], a[:, 1, h, :], ALU.mult).then_inc(s_z, 1)
                        continue
                    v = (BY_B0, BY_B1, BY_B2).index(group)
                    dve.wait_ge(s_B, 6 * k + 2 * v + h + 1)
                    for u in range(2):
                        if v == 0:
                            dve.wait_ge(s_opA, 4 * k + A_FREE + 2 * u + h + 1)
                        nc.vector.tensor_tensor(z[:, ROOM[group] + 2 * h + u, :], a[:, u, h, :],
                                                bank_B[h][0:ROWS, :], ALU.mult).then_inc(s_z, 1)

            transpose_tile(0)
            for q in range(2):
                residual(q, q)
                low_part(q, q)
            with dve.Fori(0, NTB) as t:
                for q in range(QB):
                    k = t * QB + q
                    q2 = (q + 2) % QB
                    products(k, q, BY_B0)
                    if q == 2:
                        with dve.If(t < NTB - 1):
                            dve.wait_ge(s_xcopy, k + 2)
                            transpose_tile(t + 1)
                    products(k, q, BY_B1)
                    products(k, q, SELF)
                    if q < 2:
                        residual(k + 2, q2)
                    else:
                        with dve.If(t < NTB - 1):
                            residual(k + 2, q2)
                    products(k, q, BY_B2)
                    if q < 2:
                        low_part(k + 2, q2)
                    else:
                        with dve.If(t < NTB - 1):
                            low_part(k + 2, q2)

        @block.scalar
        def _(act):
            act.sem_inc(s_opA, A_FREE)
            act.sem_inc(s_h, 1)
            act.sem_inc(s_hT, 1)
            act.sem_inc(s_pgc, PG_FREE)
            act.sem_inc(s_fc, NM)

            def copy(dst, src):
                return nc.scalar.activation(dst, src, ACT.Copy)

            def high_part(q):
                copy(part(q, 0), x_tiles(q)).then_inc(s_high, 1)

            def mid_part(k, q):
                act.wait_ge(s_resid, k + 1)
                copy(part(q, 1), resid[:, :, :]).then_inc(s_mid, 1)

            def place_x(q):
                copy(hx[:, q, :, HID:HXW], x_tiles(q))
                for g in range(G4):
                    rows = slice(g * D, (g + 1) * D)
                    last = copy(xblk[rows, q, :, g, :], x_tiles(q)[rows])
                last.then_inc(s_xcopy, 1)

            def copy_parts(k, q):
                act.wait_ge(s_partsT, k + 1)
                copy(xs[:, q % 2, :], partsT_ps[0:ROWS, :]).then_inc(s_xs, 1)

            def copy_A(k, q, u):
                for h in range(2):
                    act.wait_ge(s_A, 4 * k + 2 * u + h + 1)
                    copy(opA[:, q % 2, u, h, :], bank_A[h][0:ROWS, :]).then_inc(s_opA, 1)

            def copy_hidden(k):
                act.wait_ge(s_main, NG * (k + 1) + MAIN_FREE)
                act.wait_ge(s_ht, k + 1)
                copy(h_sb[:, :], bank_H[:, :]).then_inc(s_h, 1)

            def copy_hiddenT(k, q):
                act.wait_ge(s_ht, k + 2)
                copy(hx[:, q, :, 0:HID].rearrange("p (g t) c -> p t g c", g=2),
                     bank_T[:, :].rearrange("p (t g c) -> p t g c", t=TH, g=2)).then_inc(s_hT, 1)

            def copy_pg(k, q, i, j):
                t0, t1 = FILLS[j]
                act.wait_ge(s_pg, NF * (k + 2) + j + 1)
                src = bank_G[(NF * q + j) % 2][:, 0:(t1 - t0) * G4 * F].rearrange("p (t g f) -> p f g t", g=G4, f=F)

                def col(dst):
                    view = dst.rearrange("p f (i g t) -> p f i g t", i=TPH, g=G4)
                    view = view[:, :, bass.ds(i, 1), :, q * BLK + t0:q * BLK + t1]
                    return view.rearrange("p f i g t -> p f (i g) t")
                copy(col(pq[0:HID, :, :]), src[0:HID, 0:ILO])
                copy(col(pq[HID:P, 0:IHI, :]), src[0:HID, ILO:F])
                copy(col(gq[0:F, :, :]), src[HID:HXW, 0:ILO])
                copy(col(gq[GHI:HXW, 0:IHI, :]), src[HID:HXW, ILO:F]).then_inc(s_pgc, 1)

            for n in range(2):
                act.wait_ge(s_ctxps, n + 1)
                copy(ctxT[:, n * 512:(n + 1) * 512], bank_G[n][0:NCTX, :]).then_inc(s_ctxT, 1)
            act.wait_ge(s_xT, 1)
            high_part(0)
            mid_part(0, 0)
            copy_parts(0, 0)
            high_part(1)
            mid_part(1, 1)
            copy_A(0, 0, 0)
            copy_A(0, 0, 1)
            act.wait_ge(s_clear, 1)
            place_x(0)
            place_x(1)

            with act.Fori(0, NH) as hb:
                with act.Fori(0, TPH) as i:
                    t = hb * TPH + i
                    before = nc.s_assert_within(i - 1, 0, TPH - 1, skip_runtime_bounds_check_because="used where i > 0")
                    for q in range(QB):
                        k = t * QB + q
                        q_1, qn, q2 = (q - 1) % QB, (q + 1) % QB, (q + 2) % QB

                        def finish_before():
                            copy_hidden(k - 1)
                            if q == 0 or q >= 2:
                                copy_pg(k - 2, q2, i if q >= 2 else before, 1)
                            else:
                                with act.If(i > 0):
                                    copy_pg(k - 2, q2, before, 1)
                            copy_hiddenT(k - 1, q_1)
                            if q == 0 or q >= 2:
                                copy_pg(k - 2, q2, i if q >= 2 else before, 2)
                            else:
                                with act.If(i > 0):
                                    copy_pg(k - 2, q2, before, 2)

                        def split_ahead():
                            act.wait_ge(s_partsT, k + 1)
                            high_part(q2)

                        def copy_operands(ahead):
                            copy_A(k + 1, qn, 0)
                            if ahead:
                                mid_part(k + 2, q2)
                            copy_A(k + 1, qn, 1)
                            if ahead:
                                place_x(q2)

                        if q > 0:
                            finish_before()
                        else:
                            with act.If(i > 0):
                                finish_before()
                        if q < 2:
                            split_ahead()
                        else:
                            with act.If(t < NTB - 1):
                                if q == 2:
                                    act.wait_ge(s_xT, t + 2)
                                split_ahead()
                        if q > 0:
                            copy_pg(k - 1, q_1, i, 0)
                        else:
                            with act.If(i > 0):
                                copy_pg(k - 1, q_1, before, 0)
                        if q < 2:
                            copy_parts(k + 1, qn)
                            copy_operands(True)
                        elif q == 2:
                            copy_parts(k + 1, qn)
                            copy_A(k + 1, qn, 0)
                            with act.If(t < NTB - 1):
                                mid_part(k + 2, q2)
                            copy_A(k + 1, qn, 1)
                            with act.If(t < NTB - 1):
                                place_x(q2)
                        else:
                            with act.If(t < NTB - 1):
                                copy_parts(k + 1, qn)
                                copy_operands(True)
                last = (hb + 1) * (TPH * QB) - 1
                copy_hidden(last)
                copy_pg(last - 1, QB - 2, TPH - 1, 1)
                copy_hiddenT(last, QB - 1)
                copy_pg(last - 1, QB - 2, TPH - 1, 2)
                for j in range(NF):
                    copy_pg(last, QB - 1, TPH - 1, j)

                done = hb * NM

                def fin(n):
                    act.wait_ge(s_fin, done + n + 1)
                    return bank_G[n % 2]
                copy(c2_sb[:, :], fin(0)[0:K2, :]).then_inc(s_fc, 1)
                act.wait_ge(s_ctxT, 2)
                copy(f1_sb[FIN1:, :], ctxT[:, bass.ds(hb * HALF, HALF)])
                b1 = fin(1)
                copy(f1_sb[0:FIN1, 0:HALF // 2], b1[0:FIN1, 0:HALF // 2])
                copy(f1_sb[0:FIN1, HALF // 2:HALF], b1[64:64 + FIN1, 0:HALF // 2]).then_inc(s_fc, 1)
                act.wait_ge(s_wmlp, 16 * 7)
                for c in range(MC1):
                    nc.scalar.activation(r1[:, c, :], fin(2 + c)[:, :], ACT.Relu, bias=bt1_sb[:, c:c + 1]).then_inc(s_fc, 1)
                for c in range(MC2):
                    nc.scalar.activation(r2[:, c, :], fin(2 + MC1 + c)[:, :], ACT.Relu, bias=bt2_sb[:, c:c + 1]).then_inc(s_fc, 1)
                copy(y_sb[:, bass.ds(hb * HALF, HALF)], fin(NM - 1)[0:1, :]).then_inc(s_fc, 1)

        @block.tensor
        def _(pe):
            pe.sem_inc(s_main, MAIN_FREE)
            pe.sem_inc(s_ht, 1)
            pe.sem_inc(s_pg, 2 * NF)
            pe.sem_inc(s_z, Z_FREE)

            def matmul(dst, lhsT, rhs, first=True, last=True):
                return nc.tensor.matmul(dst, lhsT, rhs, start=first, stop=last)

            def transpose_parts(k, q):
                pe.wait_ge(s_low, k + 1)
                pe.wait_ge(s_hT, k)
                for t in range(BLK):
                    last = nc.tensor.transpose(partsT_ps[0:ROWS, t * P:(t + 1) * P], parts[:, q % 2, t, :], ident_b[:, :])
                last.then_inc(s_partsT, 1)

            def operand(n, q, h, bank, signal):
                matmul(bank[h][0:ROWS, :], sel[:, n * ROWS:(n + 1) * ROWS],
                       xs[:, q % 2, h * HALF:(h + 1) * HALF]).then_inc(signal, 1)

            def operand_A(k, q, u):
                if u == 0:
                    pe.wait_ge(s_xs, k + 1)
                for h in range(2):
                    pe.wait_ge(s_opA, 4 * k + 2 * u + h + 1)
                    operand(u, q, h, bank_A, s_A)

            def operand_B(k, q, v):
                for h in range(2):
                    pe.wait_ge(s_z, NZ * k + Z_FREE + (-2, 2, 6)[v] + 2 * h)
                    operand(2 + v, q, h, bank_B, s_B)

            def main(k, group):
                if group == BY_B0:
                    pe.wait_ge(s_h, k + 1)
                count = 2 * len(WEIGHTS[group])
                pe.wait_ge(s_z, NZ * k + Z_FREE + Z_OF[group] + count)
                for u, prod in enumerate(WEIGHTS[group]):
                    for h in range(2):
                        slot = ROOM[group] + len(WEIGHTS[group]) * h + u
                        last = matmul(bank_H[64 * h:64 * h + HID, :], w1s[:, prod, :], z[:, slot, :],
                                      first=group == BY_B0 and u == 0, last=group == BY_B2 and u == 1)
                last.then_inc(s_main, 1)

            def transpose_hidden(k):
                pe.wait_ge(s_h, k + 2)
                with_t = k + 1
                pe.wait_ge(s_xs, with_t + 1)
                for t in range(TH):
                    last = nc.tensor.transpose(bank_T[:, t * P:(t + 1) * P], h_sb[:, t * P:(t + 1) * P], ident_f[:, :])
                last.then_inc(s_ht, 1)

            def fill_pg(k, q, j):
                if j == 0:
                    pe.wait_ge(s_hT, k + 2)
                    pe.wait_ge(s_xcopy, k + 1)
                pe.wait_ge(s_pgc, NF * k + j - 1 + PG_FREE)
                for n, t in enumerate(range(*FILLS[j])):
                    last = matmul(bank_G[(NF * q + j) % 2][0:HXW, n * G4 * F:(n + 1) * G4 * F], hx[:, q, t, :],
                                  xblk[:, q, t, :, :].rearrange("p g f -> p (g f)"))
                last.then_inc(s_pg, 1)

            pe.wait_ge(s_ident, 16)
            pe.wait_ge(s_ctx, 16)
            for n in range(2):
                for t in range(NTB // 2):
                    last = nc.tensor.transpose(bank_G[n][0:NCTX, t * P:(t + 1) * P], ctx_sb[:, n * NTB // 2 + t, :], ident_f[:, :])
                last.then_inc(s_ctxps, 1)
            pe.wait_ge(s_const, 1)
            pe.wait_ge(s_ctxT, 2)
            pe.wait_ge(s_low, 1)
            for t in range(BLK):
                last = nc.tensor.transpose(partsT_ps[0:ROWS, t * P:(t + 1) * P], parts[:, 0, t, :], ident_b[:, :])
            last.then_inc(s_partsT, 1)
            operand_A(0, 0, 0)
            operand_A(0, 0, 1)
            operand_B(0, 0, 0)
            with pe.Fori(0, NH) as hb:
                with pe.Fori(0, TPH) as i:
                    t = hb * TPH + i
                    for q in range(QB):
                        k = t * QB + q
                        q_1, qn, q2 = (q - 1) % QB, (q + 1) % QB, (q + 2) % QB

                        def finish_before():
                            operand_B(k, q, 0)
                            main(k - 1, BY_B2)
                            if q == 0 or q >= 2:
                                fill_pg(k - 2, q2, 1)
                                fill_pg(k - 2, q2, 2)
                            else:
                                with pe.If(i > 0):
                                    fill_pg(k - 2, q2, 1)
                                    fill_pg(k - 2, q2, 2)
                            transpose_hidden(k - 1)

                        if q > 0:
                            finish_before()
                        else:
                            with pe.If(i > 0):
                                finish_before()
                        operand_B(k, q, 1)
                        main(k, BY_B0)
                        if q > 0:
                            fill_pg(k - 1, q_1, 0)
                        else:
                            with pe.If(i > 0):
                                fill_pg(k - 1, q_1, 0)
                        if q < QB - 1:
                            transpose_parts(k + 1, qn)
                        else:
                            with pe.If(t < NTB - 1):
                                transpose_parts(k + 1, qn)
                        operand_B(k, q, 2)
                        main(k, BY_B1)
                        if q < QB - 1:
                            operand_A(k + 1, qn, 0)
                            main(k, SELF)
                            operand_A(k + 1, qn, 1)
                        else:
                            with pe.If(t < NTB - 1):
                                operand_A(k + 1, qn, 0)
                            main(k, SELF)
                            with pe.If(t < NTB - 1):
                                operand_A(k + 1, qn, 1)
                last_k = (hb + 1) * (TPH * QB) - 1
                with pe.If(hb < NH - 1):
                    operand_B(last_k + 1, 0, 0)
                main(last_k, BY_B2)
                fill_pg(last_k - 1, QB - 2, 1)
                fill_pg(last_k - 1, QB - 2, 2)
                pe.wait_ge(s_h, last_k + 2)
                with pe.If(hb < NH - 1):
                    pe.wait_ge(s_xs, last_k + 2)
                for t in range(TH):
                    last = nc.tensor.transpose(bank_T[:, t * P:(t + 1) * P], h_sb[:, t * P:(t + 1) * P], ident_f[:, :])
                last.then_inc(s_ht, 1)
                for j in range(NF):
                    fill_pg(last_k, QB - 1, j)

                done = hb * NM
                pe.wait_ge(s_wfin, 16 * 4)
                pe.wait_ge(s_wmlp, 16 * 7)
                pe.wait_ge(s_pgc, NF * (last_k + 1) + PG_FREE)
                for f in range(ILO):
                    last = matmul(bank_G[0][:, :], w2f[:, f, :], pq[:, f, :], f == 0, f == ILO - 1)
                last.then_inc(s_fin, 1)
                for f in range(ILO):
                    for h in range(2):
                        last = matmul(bank_G[1][64 * h:64 * h + FIN1, 0:HALF // 2], w1f[:, f, :],
                                      gq[:, f, h * HALF // 2:(h + 1) * HALF // 2], f == 0, f == ILO - 1)
                last.then_inc(s_fin, 1)
                for c in range(MC1):
                    pe.wait_ge(s_fc, done + NM + max(2, 2 + c - 1))
                    cols = slice(c * P, (c + 1) * P)
                    matmul(bank_G[c % 2][:, :], wt1c[:, cols], c2_sb[:, :], True, False)
                    matmul(bank_G[c % 2][:, :], wt1f[:, cols], f1_sb[:, :], False, True).then_inc(s_fin, 1)
                for c in range(MC2):
                    pe.wait_ge(s_fc, done + NM + 2 + MC1)
                    for kc in range(MC1):
                        last = matmul(bank_G[c % 2][:, :], wt2_sb[:, kc, c * P:(c + 1) * P], r1[:, kc, :], kc == 0, kc == MC1 - 1)
                    last.then_inc(s_fin, 1)
                pe.wait_ge(s_fc, done + NM + NM - 1)
                for kc in range(MC2):
                    last = matmul(bank_G[0][0:1, :], wt3_sb[:, kc:kc + 1], r2[:, kc, :], kc == 0, kc == MC2 - 1)
                last.then_inc(s_fin, 1)
                pe.wait_ge(s_fc, done + NM + NM)


ROTATIONS = [(0, 0, 0), (19, 9, 29), (17, 0, 21), (4, 14, 28), (7, 3, 16)]
PRODUCTS = [(0, 1), (0, 2), (1, 2), (0, 3), (1, 3), (0, 4), (1, 4)]


def pair_rows(fields):
    seen, direct, swapped = set(), [], []
    for a, b in PRODUCTS:
        for ra, rb in zip(ROTATIONS[a], ROTATIONS[b]):
            distance = min((ra - rb) % fields, (rb - ra) % fields)
            new = distance not in seen
            seen.add(distance)
            for i in range(fields):
                p, q = (i + ra) % fields, (i + rb) % fields
                direct.append(p * fields + q if new else -1)
                swapped.append(q * fields + p if new and distance else -1)
    assert len(seen) == fields // 2 + 1
    return direct, swapped


def kernel(**inputs):
    import numpy as np
    import concourse.bacc as bacc
    from concourse import mybir
    from concourse.bass_utils import run_bass_kernel_spmd

    batch, fields = inputs["ids"].shape
    hidden = inputs["L0_rec_W1"].shape[1] // 2
    rows = 3 * fields

    w1 = np.asarray(inputs["L0_rec_W1"])
    padded = np.concatenate([w1[:, :hidden], np.zeros((1, hidden), w1.dtype)])
    w1a, w1b = (np.ascontiguousarray(padded[np.array(r)].reshape(len(PRODUCTS), rows, hidden).transpose(1, 0, 2))
                for r in pair_rows(fields))
    select = np.zeros((3, fields, 5, 3, fields), np.float32)
    for n, rots in enumerate(ROTATIONS):
        for r, off in enumerate(rots):
            for i in range(fields):
                select[:, (i + off) % fields, n, r, i] = 1.0

    arrays = {"dense_ctx": inputs["dense_ctx"], "ids": inputs["ids"]}
    arrays.update({f"tbl_{f}": inputs[f"tbl_{f}"] for f in range(fields)})
    arrays.update({"w1a": w1a, "w1b": w1b, "select": select.reshape(rows, 5 * rows), "ident": np.eye(128, dtype=np.float32),
                   "w1": w1, "w2": inputs["L0_rec_W2"], "wt1": inputs["W_top1"], "bt1": inputs["b_top1"],
                   "wt2": inputs["W_top2"], "bt2": inputs["b_top2"], "wt3": inputs["W_top3"]})
    nc = bacc.Bacc("TRN2", target_bir_lowering=False, num_devices=1)
    feeds, aps = {}, {}
    for name, a in arrays.items():
        a = np.ascontiguousarray(a)
        feeds[f"in_{name}"] = a
        aps[name] = nc.dram_tensor(f"in_{name}", a.shape, mybir.dt.from_np(a.dtype), kind="ExternalInput").ap()
    out = nc.dram_tensor("out_y", (batch, 1), mybir.dt.float32, kind="ExternalOutput").ap()
    build(nc, aps["dense_ctx"], aps["ids"], [aps[f"tbl_{f}"] for f in range(fields)], aps["w1a"], aps["w1b"],
          aps["select"], aps["ident"], aps["w1"], aps["w2"], aps["wt1"], aps["bt1"], aps["wt2"], aps["bt2"], aps["wt3"], out)
    result = run_bass_kernel_spmd(nc, [feeds], core_ids=[0])
    return result.results[0]["out_y"]
```

```python
def build(nc, dense_ctx, ids, tables, w1a, w1b, select, ident, w1, w2, wt1, bt1, wt2, bt2, wt3, out):
    from contextlib import ExitStack, nullcontext

    import concourse.bass as bass
    from concourse import mybir

    FP32 = mybir.dt.float32
    BF16 = mybir.dt.bfloat16
    I32 = mybir.dt.int32
    ALU = mybir.AluOpType
    ACT = mybir.ActivationFunctionType

    BATCH, F = ids.shape
    D = tables[0].shape[1]
    NCTX = dense_ctx.shape[1]
    K1 = w1.shape[1]
    HID = K1 // 2
    FIN1 = K1 - HID
    K2 = w2.shape[1]
    M1, M2 = wt2.shape
    PROWS = select.shape[0]
    ROWS = w1a.shape[0]
    NP = w1a.shape[1]
    P = 128
    G4 = P // D
    TB = P
    NTB = BATCH // TB
    TILES = TB // G4
    BLK = 8
    QB = TILES // BLK
    HALF = 512
    TH = HALF // P
    NH = BATCH // HALF
    TPH = NTB // NH
    ILO = (F + 1) // 2
    IHI = F - ILO
    THIRD = F // 3
    GPACK = [(0, F, 2 * THIRD), (64, 2 * THIRD, THIRD), (96, THIRD, 0)]
    GROWS = 96 + THIRD
    HXW = HID + F
    FILLS = [(0, 3), (3, 6), (6, 8)]
    NF = len(FILLS)
    NZ = 2 * NP
    PRODUCTS = product_operands()
    B = 3
    BY_A0, BY_A2, A2_B, BY_B = range(4)
    WEIGHTS = [(0, 1), (2, 3), (4,), (5, 6)]
    NG = 4
    Z_OF = [0, 4, 8, 10]
    ROOM = [0, 4, 0, 8]
    ROOM_AFTER = [-1, -2, 1, 0]
    MC1, MC2 = M1 // P, M2 // P
    NM = 2 + MC1 + MC2 + 1
    Z_FREE, MAIN_FREE, A_FREE, PG_FREE = 4, NG, 2, 2 + 2 * NF

    with ExitStack() as ctx:
        def sb(name, shape, dt=FP32):
            return ctx.enter_context(nc.sbuf_tensor(name, shape, dt))

        def pb(name):
            return ctx.enter_context(nc.psum_tensor(name, [P, 512], FP32))

        def sem(name):
            return ctx.enter_context(nc.semaphore(name))

        ids_sb = sb("ids_sb", [P, NTB, F], I32)
        idx = sb("idx", [P, 2, F], I32)
        ident_f = sb("ident_f", [P, P])
        ident_b = sb("ident_b", [P, P], BF16)
        sel = sb("sel", [PROWS, 4 * ROWS], BF16)
        w1s = sb("w1s", [ROWS, NP, HID])
        w2f = sb("w2f", [P, ILO, K2])
        w1f = sb("w1f", [GROWS, THIRD, FIN1])
        wt1c = sb("wt1c", [K2, M1])
        wt1f = sb("wt1f", [FIN1 + NCTX, M1])
        wt2_sb = sb("wt2_sb", [P, MC1, M2])
        wt3_sb = sb("wt3_sb", [P, MC2])
        bt1_sb = sb("bt1_sb", [P, MC1])
        bt2_sb = sb("bt2_sb", [P, MC2])
        ctx_sb = sb("ctx_sb", [P, NTB, NCTX])
        gath = sb("gath", [P, 2, F, D])
        xT = sb("xT", [P, F, TILES])
        resid = sb("resid", [P, BLK, F])
        parts = sb("parts", [P, 2, BLK, PROWS], BF16)
        xs = sb("xs", [PROWS, 2, 2 * HALF], BF16)
        hx = sb("hx", [P, QB, BLK, HXW])
        xblk = sb("xblk", [P, QB, BLK, G4, F])
        opA = sb("opA", [ROWS, 2, 3, 2, HALF])
        z = sb("z", [ROWS, 3 * 4, HALF])
        h_sb = sb("h_sb", [P, HALF])
        pq = sb("pq", [P, ILO, HALF])
        gq = sb("gq", [GROWS, THIRD, HALF])
        f1_sb = sb("f1_sb", [FIN1 + NCTX, HALF])
        rows_sb = sb("rows_sb", [FIN1 + NCTX, BATCH])
        ctxT = rows_sb[FIN1:, :]
        y_sb = rows_sb[0:1, :]
        w1a_sb = pq[0:ROWS, 8, 0:NP * HID].rearrange("p (n k) -> p n k", n=NP)
        w1b_sb = pq[0:ROWS, 9, 0:NP * HID].rearrange("p (n k) -> p n k", n=NP)
        sel_f = pq[0:PROWS, 10, 0:4 * ROWS]
        w1f_swap = pq[0:64 + THIRD, 12:14, :].rearrange("p a n -> p (a n)")[:, 0:THIRD * FIN1].rearrange("p (s k) -> p s k", k=FIN1)
        r1 = pq[:, 0:MC1, :]
        r2 = pq[:, MC1:MC1 + MC2, :]
        c2_sb = pq[0:K2, MC1 + MC2, :]

        bank_T = pb("bank_T")
        bank_A = [pb("bank_A0"), pb("bank_A1")]
        bank_B = [pb("bank_B0"), pb("bank_B1")]
        bank_H = pb("bank_H")
        bank_G = [pb("bank_G0"), pb("bank_G1")]
        partsT_ps = bank_T[:, :].bitcast(BF16)

        s_ids = sem("s_ids")
        s_sel = sem("s_sel")
        s_ident = sem("s_ident")
        s_w1 = sem("s_w1")
        s_ctx = sem("s_ctx")
        s_wfin = sem("s_wfin")
        s_w1f = sem("s_w1f")
        s_wmlp = sem("s_wmlp")
        s_gath = [sem("s_gath0"), sem("s_gath1")]
        s_out = sem("s_out")
        s_const = sem("s_const")
        s_clear = sem("s_clear")
        s_xT = sem("s_xT")
        s_resid = sem("s_resid")
        s_low = sem("s_low")
        s_z = sem("s_z")
        s_idx = sem("s_idx")
        s_issue = sem("s_issue")
        s_high = sem("s_high")
        s_mid = sem("s_mid")
        s_xcopy = sem("s_xcopy")
        s_xs = sem("s_xs")
        s_opA = sem("s_opA")
        s_h = sem("s_h")
        s_hT = sem("s_hT")
        s_pgc = sem("s_pgc")
        s_ctxT = sem("s_ctxT")
        s_fc = sem("s_fc")
        s_ctxps = sem("s_ctxps")
        s_partsT = sem("s_partsT")
        s_A = sem("s_A")
        s_B = sem("s_B")
        s_main = sem("s_main")
        s_ht = sem("s_ht")
        s_pg = sem("s_pg")
        s_fin = sem("s_fin")

        block = ctx.enter_context(nc.Block())

        @block.sync
        def _(sp):
            sp.dma_start(ids_sb[:, :, :], ids.rearrange("(t p) f -> p t f", p=P)).then_inc(s_ids, 16)
            sp.dma_start(ident_f[:, :], ident).then_inc(s_ident, 16)
            sp.dma_start(sel_f[:, :], select).then_inc(s_sel, 16)
            sp.dma_start(w1a_sb[:, :, :], w1a).then_inc(s_w1, 16)
            sp.dma_start(w1b_sb[:, :, :], w1b).then_inc(s_w1, 16)
            sp.dma_start(ctx_sb[:, :, :], dense_ctx.rearrange("(t p) c -> p t c", p=P)).then_inc(s_ctx, 16)
            w2v = w2.rearrange("(i j) m -> j i m", j=HID)
            sp.wait_ge(s_clear, 1)
            sp.dma_start(w2f[0:HID, :, :], w2v[:, 0:ILO, :]).then_inc(s_wfin, 16)
            sp.dma_start(w2f[HID:P, 0:IHI, :], w2v[:, ILO:F, :]).then_inc(s_wfin, 16)
            w1v = w1.rearrange("(c i) k -> c i k", i=F)
            for p0, n, i0 in GPACK:
                sp.dma_start(w1f[p0:p0 + n, :, :], w1v[0:n, i0:i0 + THIRD, HID:K1]).then_inc(s_w1f, 16)
            w1t = w1.rearrange("(i c) k -> c i k", c=F)
            for p0, n, i0 in GPACK[:2]:
                sp.dma_start(w1f_swap[p0:p0 + i0, :, :], w1t[0:i0, i0:i0 + THIRD, HID:K1]).then_inc(s_w1f, 16)
            sp.dma_start(wt1c[:, :], wt1[FIN1:FIN1 + K2, :]).then_inc(s_wmlp, 16)
            sp.dma_start(wt1f[0:FIN1, :], wt1[0:FIN1, :]).then_inc(s_wmlp, 16)
            sp.dma_start(wt1f[FIN1:, :], wt1[FIN1 + K2:, :]).then_inc(s_wmlp, 16)
            sp.dma_start(wt2_sb[:, :, :], wt2.rearrange("(c p) m -> p c m", p=P)).then_inc(s_wmlp, 16)
            with nc.allow_non_contiguous_dma("three small vectors"):
                sp.dma_start(wt3_sb[:, :], wt3.rearrange("(c p) o -> p (c o)", p=P)).then_inc(s_wmlp, 16)
                sp.dma_start(bt1_sb[:, :], bt1.rearrange("(c p) -> p c", p=P)).then_inc(s_wmlp, 16)
                sp.dma_start(bt2_sb[:, :], bt2.rearrange("(c p) -> p c", p=P)).then_inc(s_wmlp, 16)
            sp.wait_ge(s_fc, NM * (NH + 1))
            sp.dma_start(out.rearrange("b o -> o b"), y_sb[:, :]).then_inc(s_out, 16)
            sp.wait_ge(s_out, 16)

        @block.gpsimd
        def _(pool):
            def gather(slot, indices):
                for f in range(F):
                    pool.indirect_dma_start(
                        out=gath[:, slot, f, :], out_offset=None, in_=tables[f],
                        in_offset=bass.IndirectOffsetOnAxis(ap=indices[:, f:f + 1], axis=0)).then_inc(s_gath[slot], 16)

            pool.wait_ge(s_ids, 16)
            pool.sem_inc(s_issue, 1)
            gather(0, ids_sb[:, 0, :])
            gather(1, ids_sb[:, 1, :])
            with pool.Fori(1, NTB // 2) as n:
                for slot in range(2):
                    t = n * 2 + slot
                    pool.wait_ge(s_xT, t - 1)
                    nc.gpsimd.tensor_copy(idx[:, slot, :], ids_sb[:, bass.ds(t, 1), :].rearrange("p a f -> p (a f)")).then_inc(s_idx, 1)
                    pool.wait_ge(s_idx, t - 1)
                    pool.sem_inc(s_issue, 1)
                    gather(slot, idx[:, slot, :])

        def x_tiles(q):
            return xT[:, :, q * BLK:(q + 1) * BLK].rearrange("p f t -> p t f")

        def part(q, n):
            return parts[:, q % 2, :, n * F:(n + 1) * F]

        @block.vector
        def _(dve):
            dve.wait_ge(s_ident, 16)
            nc.vector.tensor_copy(ident_b[:, :], ident_f[:, :])
            dve.wait_ge(s_sel, 16)
            nc.vector.tensor_copy(sel[:, :], sel_f[:, :])
            dve.wait_ge(s_w1, 32)
            nc.vector.tensor_tensor(w1s[:, :, :], w1a_sb[:, :, :], w1b_sb[:, :, :], ALU.add).then_inc(s_const, 1)
            nc.vector.memset(xblk[:, :, :, :, :], 0.0)
            nc.vector.memset(gq[:, :, :], 0.0)
            nc.vector.memset(w1f[:, :, :], 0.0)
            nc.vector.memset(w2f[HID:P, IHI:ILO, :], 0.0)
            nc.vector.memset(pq[HID:P, IHI:ILO, :], 0.0).then_inc(s_clear, 1)

            dve.wait_ge(s_w1f, 16 * 5)
            for n, (p0, _, i0) in enumerate(GPACK[:2]):
                nc.vector.tensor_tensor(w1f[p0:p0 + i0, :, :], w1f[p0:p0 + i0, :, :], w1f_swap[p0:p0 + i0, :, :],
                                        ALU.add).then_inc(s_const, 1)

            def transpose_tile(slot):
                nc.vector.transpose(xT[:, :, :].rearrange("p f t -> p (f t)"),
                                    gath[:, slot, :, :].rearrange("p f d -> p (f d)")).then_inc(s_xT, 1)

            def residual(k, q):
                dve.wait_ge(s_high, k + 1)
                if not (isinstance(k, int) and k == 0):
                    dve.wait_ge(s_low, k)
                nc.vector.tensor_tensor(resid[:, :, :], x_tiles(q), part(q, 0), ALU.subtract).then_inc(s_resid, 1)

            def low_part(k, q):
                dve.wait_ge(s_mid, k + 1)
                nc.vector.tensor_tensor(part(q, 2), resid[:, :, :], part(q, 1), ALU.subtract).then_inc(s_low, 1)

            def products(k, q, group):
                a = opA[:, q % 2, :, :, :]
                dve.wait_ge(s_main, NG * k + ROOM_AFTER[group] + MAIN_FREE)
                for h in range(2):
                    if group == BY_A0:
                        dve.wait_ge(s_opA, 6 * k + A_FREE + 2 + h + 1)
                    elif group == BY_A2:
                        dve.wait_ge(s_opA, 6 * k + A_FREE + 4 + h + 1)
                    elif group == A2_B:
                        dve.wait_ge(s_B, 2 * k + h + 1)
                    for u, n in enumerate(WEIGHTS[group]):
                        x, y = PRODUCTS[n]
                        nc.vector.tensor_tensor(z[:, ROOM[group] + len(WEIGHTS[group]) * h + u, :], a[:, x, h, :],
                                                bank_B[h][:, :] if y == B else a[:, y, h, :], ALU.mult).then_inc(s_z, 1)

            dve.wait_ge(s_gath[0], 16 * F)
            transpose_tile(0)
            for q in range(2):
                dve.wait_ge(s_xT, 1)
                nc.vector.tensor_copy(part(q, 0), x_tiles(q)).then_inc(s_high, 1)
                residual(q, q)
                dve.wait_ge(s_resid, q + 1)
                nc.vector.tensor_copy(part(q, 1), resid[:, :, :]).then_inc(s_mid, 1)
                low_part(q, q)
            def next_tile(n, slot, t):
                dve.wait_ge(s_xcopy, t * QB + 4)
                dve.wait_ge(s_gath[1 - slot], (n + slot + 1) * (16 * F))
                transpose_tile(1 - slot)

            with dve.Fori(0, NTB // 2) as n:
                for slot in range(2):
                    t = n * 2 + slot

                    def if_next():
                        return dve.If(n < NTB // 2 - 1) if slot else nullcontext()

                    for q in range(QB):
                        k = t * QB + q
                        q2 = (q + 2) % QB
                        products(k, q, BY_A0)
                        if q == 2:
                            with dve.If(n < NTB // 2 - 1) if slot else dve.If(n > 0):
                                next_tile(n, slot, t)
                        products(k, q, BY_A2)
                        products(k, q, A2_B)
                        if q < 2:
                            residual(k + 2, q2)
                        elif q == 3 or slot == 1:
                            with if_next():
                                residual(k + 2, q2)
                        else:
                            with dve.If(n > 0):
                                residual(k + 2, q2)
                            with dve.If(n == 0):
                                next_tile(n, slot, t)
                        products(k, q, BY_B)
                        if q == 2 and slot == 0:
                            with dve.If(n == 0):
                                residual(k + 2, q2)
                        if q < 2:
                            low_part(k + 2, q2)
                        else:
                            with if_next():
                                low_part(k + 2, q2)

        @block.scalar
        def _(act):
            act.sem_inc(s_opA, A_FREE)
            act.sem_inc(s_h, 1)
            act.sem_inc(s_hT, 1)
            act.sem_inc(s_pgc, PG_FREE)
            act.sem_inc(s_fc, NM)

            def copy(dst, src):
                return nc.scalar.activation(dst, src, ACT.Copy)

            def high_part(q):
                copy(part(q, 0), x_tiles(q)).then_inc(s_high, 1)

            def mid_part(k, q):
                act.wait_ge(s_resid, k + 1)
                copy(part(q, 1), resid[:, :, :]).then_inc(s_mid, 1)

            def place_x(q):
                copy(hx[:, q, :, HID:HXW], x_tiles(q))
                for g in range(G4):
                    rows = slice(g * D, (g + 1) * D)
                    last = copy(xblk[rows, q, :, g, :], x_tiles(q)[rows])
                last.then_inc(s_xcopy, 1)

            def copy_parts(k, q):
                act.wait_ge(s_partsT, k + 1)
                copy(xs[:, q % 2, :], partsT_ps[0:PROWS, :]).then_inc(s_xs, 1)

            def copy_A(k, q, u):
                for h in range(2):
                    act.wait_ge(s_A, 6 * k + 2 * u + h + 1)
                    copy(opA[:, q % 2, u, h, :], bank_A[h][:, :]).then_inc(s_opA, 1)

            def copy_hidden(k):
                act.wait_ge(s_main, NG * (k + 1) + MAIN_FREE)
                act.wait_ge(s_ht, k + 1)
                copy(h_sb[:, :], bank_H[:, :]).then_inc(s_h, 1)

            def copy_hiddenT(k, q):
                act.wait_ge(s_ht, k + 2)
                copy(hx[:, q, :, 0:HID].rearrange("p (g t) c -> p t g c", g=2),
                     bank_T[:, :].rearrange("p (t g c) -> p t g c", t=TH, g=2)).then_inc(s_hT, 1)

            def copy_pg(k, q, i, j):
                t0, t1 = FILLS[j]
                act.wait_ge(s_pg, NF * (k + 2) + j + 1)
                src = bank_G[(NF * q + j) % 2][:, 0:(t1 - t0) * G4 * F].rearrange("p (t g f) -> p f g t", g=G4, f=F)

                def col(dst):
                    view = dst.rearrange("p f (i g t) -> p f i g t", i=TPH, g=G4)
                    view = view[:, :, bass.ds(i, 1), :, q * BLK + t0:q * BLK + t1]
                    return view.rearrange("p f i g t -> p f (i g) t")
                copy(col(pq[0:HID, :, :]), src[0:HID, 0:ILO])
                copy(col(pq[HID:P, 0:IHI, :]), src[0:HID, ILO:F])
                for p0, n, i0 in GPACK:
                    last = copy(col(gq[p0:p0 + n, :, :]), src[HID:HID + n, i0:i0 + THIRD])
                last.then_inc(s_pgc, 1)

            for n in range(2):
                act.wait_ge(s_ctxps, n + 1)
                copy(ctxT[:, n * 512:(n + 1) * 512], bank_G[n][0:NCTX, :]).then_inc(s_ctxT, 1)
            copy_parts(0, 0)
            copy_A(0, 0, 0)
            copy_A(0, 0, 1)
            copy_A(0, 0, 2)
            act.wait_ge(s_clear, 1)
            place_x(0)
            place_x(1)
            act.wait_ge(s_low, 2)

            with act.Fori(0, NH) as hb:
                with act.Fori(0, TPH) as i:
                    t = hb * TPH + i
                    before = nc.s_assert_within(i - 1, 0, TPH - 1, skip_runtime_bounds_check_because="used where i > 0")
                    for q in range(QB):
                        k = t * QB + q
                        q_1, qn, q2 = (q - 1) % QB, (q + 1) % QB, (q + 2) % QB

                        def finish_before():
                            copy_hidden(k - 1)
                            copy_A(k, q, 2)
                            if q == 0 or q >= 2:
                                copy_pg(k - 2, q2, i if q >= 2 else before, 1)
                            else:
                                with act.If(i > 0):
                                    copy_pg(k - 2, q2, before, 1)
                            copy_hiddenT(k - 1, q_1)
                            if q == 0 or q >= 2:
                                copy_pg(k - 2, q2, i if q >= 2 else before, 2)
                            else:
                                with act.If(i > 0):
                                    copy_pg(k - 2, q2, before, 2)

                        def split_ahead():
                            act.wait_ge(s_partsT, k + 1)
                            high_part(q2)

                        def copy_operands(ahead):
                            copy_A(k + 1, qn, 0)
                            if ahead:
                                mid_part(k + 2, q2)
                            copy_A(k + 1, qn, 1)
                            if ahead:
                                place_x(q2)

                        if q > 0:
                            finish_before()
                        else:
                            with act.If(i > 0):
                                finish_before()
                        if q < 2:
                            split_ahead()
                        elif q == 2:
                            with act.If(t > 0):
                                with act.If(t < NTB - 1):
                                    act.wait_ge(s_xT, t + 2)
                                    split_ahead()
                        else:
                            with act.If(t < NTB - 1):
                                split_ahead()
                        if q < QB - 1:
                            copy_parts(k + 1, qn)
                        else:
                            with act.If(t < NTB - 1):
                                copy_parts(k + 1, qn)
                        if q > 0:
                            copy_pg(k - 1, q_1, i, 0)
                        else:
                            with act.If(i > 0):
                                copy_pg(k - 1, q_1, before, 0)
                        if q < 2:
                            copy_operands(True)
                        elif q == 2:
                            copy_A(k + 1, qn, 0)
                            with act.If(t > 0):
                                with act.If(t < NTB - 1):
                                    mid_part(k + 2, q2)
                            copy_A(k + 1, qn, 1)
                            with act.If(t == 0):
                                act.wait_ge(s_xT, 2)
                                split_ahead()
                                mid_part(k + 2, q2)
                            with act.If(t < NTB - 1):
                                place_x(q2)
                        else:
                            with act.If(t < NTB - 1):
                                copy_operands(True)
                last = (hb + 1) * (TPH * QB) - 1
                copy_hidden(last)
                with act.If(hb < NH - 1):
                    copy_A(last + 1, 0, 2)
                copy_pg(last - 1, QB - 2, TPH - 1, 1)
                copy_hiddenT(last, QB - 1)
                copy_pg(last - 1, QB - 2, TPH - 1, 2)
                for j in range(NF):
                    copy_pg(last, QB - 1, TPH - 1, j)

                done = hb * NM

                def fin(n):
                    act.wait_ge(s_fin, done + n + 1)
                    return bank_H if n == 0 else bank_G[n % 2]
                act.wait_ge(s_ctxT, 2)
                copy(f1_sb[FIN1:, :], ctxT[:, bass.ds(hb * HALF, HALF)])
                copy(c2_sb[:, :], fin(0)[0:K2, :]).then_inc(s_fc, 1)
                b1 = fin(1)
                copy(f1_sb[0:FIN1, 0:HALF // 2], b1[0:FIN1, 0:HALF // 2])
                copy(f1_sb[0:FIN1, HALF // 2:HALF], b1[64:64 + FIN1, 0:HALF // 2]).then_inc(s_fc, 1)
                act.wait_ge(s_wmlp, 16 * 7)
                for c in range(MC1):
                    nc.scalar.activation(r1[:, c, :], fin(2 + c)[:, :], ACT.Relu, bias=bt1_sb[:, c:c + 1]).then_inc(s_fc, 1)
                for c in range(MC2):
                    nc.scalar.activation(r2[:, c, :], fin(2 + MC1 + c)[:, :], ACT.Relu, bias=bt2_sb[:, c:c + 1]).then_inc(s_fc, 1)
                copy(y_sb[:, bass.ds(hb * HALF, HALF)], fin(NM - 1)[0:1, :]).then_inc(s_fc, 1)

        @block.tensor
        def _(pe):
            pe.sem_inc(s_main, MAIN_FREE)
            pe.sem_inc(s_ht, 1)
            pe.sem_inc(s_pg, 2 * NF)
            pe.sem_inc(s_z, Z_FREE)

            def matmul(dst, lhsT, rhs, first=True, last=True):
                return nc.tensor.matmul(dst, lhsT, rhs, start=first, stop=last)

            def transpose_parts(k, q):
                pe.wait_ge(s_low, k + 1)
                pe.wait_ge(s_hT, k)
                for t in range(BLK):
                    last = nc.tensor.transpose(partsT_ps[0:PROWS, t * P:(t + 1) * P], parts[:, q % 2, t, :], ident_b[:, :])
                last.then_inc(s_partsT, 1)

            def operand(n, q, h, bank, signal):
                matmul(bank[h][:, :], sel[:, n * ROWS:(n + 1) * ROWS],
                       xs[:, q % 2, h * HALF:(h + 1) * HALF]).then_inc(signal, 1)

            def operand_A(k, q, u):
                if u == 0:
                    pe.wait_ge(s_xs, k + 1)
                for h in range(2):
                    pe.wait_ge(s_opA, 6 * k + 2 * u + h + 1)
                    operand(u, q, h, bank_A, s_A)

            def operand_B(k, q):
                for h in range(2):
                    pe.wait_ge(s_z, NZ * k + Z_FREE - 2 + 2 * h)
                    operand(B, q, h, bank_B, s_B)

            def main(k, group):
                if group == BY_A0:
                    pe.wait_ge(s_h, k + 1)
                count = 2 * len(WEIGHTS[group])
                pe.wait_ge(s_z, NZ * k + Z_FREE + Z_OF[group] + count)
                for u, prod in enumerate(WEIGHTS[group]):
                    for h in range(2):
                        slot = ROOM[group] + len(WEIGHTS[group]) * h + u
                        last = matmul(bank_H[64 * h:64 * h + HID, :], w1s[:, prod, :], z[:, slot, :],
                                      first=group == BY_A0 and u == 0, last=group == BY_B and u == 1)
                last.then_inc(s_main, 1)

            def transpose_hidden(k):
                pe.wait_ge(s_h, k + 2)
                with_t = k + 1
                pe.wait_ge(s_xs, with_t + 1)
                for t in range(TH):
                    last = nc.tensor.transpose(bank_T[:, t * P:(t + 1) * P], h_sb[:, t * P:(t + 1) * P], ident_f[:, :])
                last.then_inc(s_ht, 1)

            def fill_pg(k, q, j):
                if j == 0:
                    pe.wait_ge(s_hT, k + 2)
                    pe.wait_ge(s_xcopy, k + 1)
                pe.wait_ge(s_pgc, NF * k + j - 1 + PG_FREE)
                for n, t in enumerate(range(*FILLS[j])):
                    last = matmul(bank_G[(NF * q + j) % 2][0:HXW, n * G4 * F:(n + 1) * G4 * F], hx[:, q, t, :],
                                  xblk[:, q, t, :, :].rearrange("p g f -> p (g f)"))
                last.then_inc(s_pg, 1)

            pe.wait_ge(s_ident, 16)
            pe.wait_ge(s_ctx, 16)
            for n in range(2):
                for t in range(NTB // 2):
                    last = nc.tensor.transpose(bank_G[n][0:NCTX, t * P:(t + 1) * P], ctx_sb[:, n * NTB // 2 + t, :], ident_f[:, :])
                last.then_inc(s_ctxps, 1)
            pe.wait_ge(s_const, 3)
            pe.wait_ge(s_ctxT, 2)
            pe.wait_ge(s_low, 1)
            for t in range(BLK):
                last = nc.tensor.transpose(partsT_ps[0:PROWS, t * P:(t + 1) * P], parts[:, 0, t, :], ident_b[:, :])
            last.then_inc(s_partsT, 1)
            operand_A(0, 0, 0)
            operand_A(0, 0, 1)
            operand_A(0, 0, 2)
            with pe.Fori(0, NH) as hb:
                with pe.Fori(0, TPH) as i:
                    t = hb * TPH + i
                    for q in range(QB):
                        k = t * QB + q
                        q_1, qn, q2 = (q - 1) % QB, (q + 1) % QB, (q + 2) % QB

                        def finish_before():
                            main(k - 1, BY_B)
                            operand_A(k, q, 2)
                            if q == 0 or q >= 2:
                                fill_pg(k - 2, q2, 1)
                                fill_pg(k - 2, q2, 2)
                            else:
                                with pe.If(i > 0):
                                    fill_pg(k - 2, q2, 1)
                                    fill_pg(k - 2, q2, 2)
                            transpose_hidden(k - 1)

                        if q > 0:
                            finish_before()
                        else:
                            with pe.If(i > 0):
                                finish_before()
                        main(k, BY_A0)
                        operand_B(k, q)
                        if q > 0:
                            if q == 1:
                                pe.wait_ge(s_fc, NM * (hb + 1))
                            fill_pg(k - 1, q_1, 0)
                        else:
                            with pe.If(i > 0):
                                fill_pg(k - 1, q_1, 0)
                        if q < QB - 1:
                            transpose_parts(k + 1, qn)
                        else:
                            with pe.If(t < NTB - 1):
                                transpose_parts(k + 1, qn)
                        main(k, BY_A2)
                        if q < QB - 1:
                            operand_A(k + 1, qn, 0)
                            main(k, A2_B)
                            operand_A(k + 1, qn, 1)
                        else:
                            with pe.If(t < NTB - 1):
                                operand_A(k + 1, qn, 0)
                            main(k, A2_B)
                            with pe.If(t < NTB - 1):
                                operand_A(k + 1, qn, 1)
                last_k = (hb + 1) * (TPH * QB) - 1
                before_last = slice(0, (TPH - 1) * P)

                def conv2(fields, cols):
                    for f in fields:
                        last = matmul(bank_H[0:K2, cols], w2f[:, f, :], pq[:, f, cols], f == 0, f == ILO - 1)
                    return last
                main(last_k, BY_B)
                with pe.If(hb < NH - 1):
                    operand_A(last_k + 1, 0, 2)
                fill_pg(last_k - 1, QB - 2, 1)
                fill_pg(last_k - 1, QB - 2, 2)
                pe.wait_ge(s_h, last_k + 2)
                with pe.If(hb < NH - 1):
                    pe.wait_ge(s_xs, last_k + 2)
                for t in range(TH):
                    last = nc.tensor.transpose(bank_T[:, t * P:(t + 1) * P], h_sb[:, t * P:(t + 1) * P], ident_f[:, :])
                last.then_inc(s_ht, 1)
                pe.wait_ge(s_wfin, 16 * 2)
                pe.wait_ge(s_pgc, NF * (last_k - QB + 1) + PG_FREE)
                conv2(range(0, 2), before_last)
                fill_pg(last_k, QB - 1, 0)
                conv2(range(2, 4), before_last)
                fill_pg(last_k, QB - 1, 1)
                conv2(range(4, 6), before_last)
                fill_pg(last_k, QB - 1, 2)
                conv2(range(6, ILO), before_last)

                done = hb * NM
                pe.wait_ge(s_pgc, NF * (last_k + 1) + PG_FREE)
                conv2(range(ILO), slice((TPH - 1) * P, HALF)).then_inc(s_fin, 1)
                for f in range(THIRD):
                    for h in range(2):
                        last = matmul(bank_G[1][64 * h:64 * h + FIN1, 0:HALF // 2], w1f[:, f, :],
                                      gq[:, f, h * HALF // 2:(h + 1) * HALF // 2], f == 0, f == THIRD - 1)
                last.then_inc(s_fin, 1)
                pe.wait_ge(s_wmlp, 16 * 7)

                def copied(n):
                    pe.wait_ge(s_fc, done + NM + n)
                for c in range(MC1):
                    cols = slice(c * P, (c + 1) * P)
                    copied(1 + c)
                    matmul(bank_G[c % 2][:, :], wt1c[:, cols], c2_sb[:, :], True, False)
                    if c == 0:
                        copied(2)
                    matmul(bank_G[c % 2][:, :], wt1f[:, cols], f1_sb[:, :], False, True).then_inc(s_fin, 1)
                for c in range(MC2):
                    n = 2 + MC1 + c
                    for kc in range(MC1):
                        if c == 0:
                            copied(max(3 + kc, n - 1))
                        elif kc == 0:
                            copied(n - 1)
                        last = matmul(bank_G[n % 2][:, :], wt2_sb[:, kc, c * P:(c + 1) * P], r1[:, kc, :], kc == 0, kc == MC1 - 1)
                    last.then_inc(s_fin, 1)
                for kc in range(MC2):
                    copied(max(3 + MC1 + kc, NM - 2))
                    last = matmul(bank_G[(NM - 1) % 2][0:1, :], wt3_sb[:, kc:kc + 1], r2[:, kc, :], kc == 0, kc == MC2 - 1)
                last.then_inc(s_fin, 1)


QUADS = [
    (18, 30, 10, 21), (24, 12, 6, 25), (36, 17, 8, 23), (35, 33, 3, 32), (34, 28, 1, 27), (1, 6, 31, 33), (12, 7, 14, 20),
    (10, 3, 29, 6), (5, 20, 30, 1), (36, 25, 28, 18), (23, 35, 6, 26), (8, 4, 2, 6), (10, 0, 11, 13), (12, 21, 31, 27),
    (3, 23, 15, 16), (28, 3, 21, 14), (26, 17, 0, 20), (2, 13, 15, 20), (26, 5, 4, 18), (17, 9, 27, 3), (33, 19, 28, 38),
    (1, 13, 16, 35), (17, 38, 10, 7), (10, 8, 27, 19), (22, 3, 38, 0), (20, 10, 37, 23), (11, 24, 31, 32), (18, 22, 33, 20),
    (6, 17, 32, 18), (12, 3, 36, 35), (35, 22, 14, 10), (24, 13, 29, 17), (24, 28, 37, 0), (26, 9, 33, 15), (31, 28, 30, 17),
    (38, 30, 12, 24), (17, 6, 37, 34), (37, 30, 13, 3), (25, 23, 21, 0), (0, 36, 9, 31), (11, 26, 34, 3), (32, 8, 29, 21),
]
EXTRA_QUADS = [(36, 37, 38, 0), (0, 1, 2, 3)]


def product_operands():
    return [(0, 0), (0, 1), (0, 2), (1, 2), (2, 3), (0, 3), (1, 3)]


def quadruples(fields):
    def move(f, by):
        return f if f >= fields - 3 else f // 3 * 3 + (f + by) % 3
    assert fields == 39
    return [tuple(move(f, by) for f in quad) for quad in QUADS for by in range(3)] + EXTRA_QUADS


def pair_rows(fields):
    seen, direct, swapped = set(), [], []
    for a, b in product_operands():
        for quad in quadruples(fields):
            p, q = quad[a], quad[b]
            new = (p, q) not in seen
            seen.update([(p, q), (q, p)])
            direct.append(p * fields + q if new else -1)
            swapped.append(q * fields + p if new and p != q else -1)
    assert len(seen) == fields * fields
    return direct, swapped


def kernel(**inputs):
    import numpy as np
    import concourse.bacc as bacc
    from concourse import mybir
    from concourse.bass_utils import run_bass_kernel_spmd

    batch, fields = inputs["ids"].shape
    hidden = inputs["L0_rec_W1"].shape[1] // 2
    quads = quadruples(fields)
    rows = len(quads)

    w1 = np.asarray(inputs["L0_rec_W1"])
    padded = np.concatenate([w1[:, :hidden], np.zeros((1, hidden), w1.dtype)])
    w1a, w1b = (np.ascontiguousarray(padded[np.array(r)].reshape(-1, rows, hidden).transpose(1, 0, 2))
                for r in pair_rows(fields))
    select = np.zeros((3, fields, 4, rows), np.float32)
    for r, quad in enumerate(quads):
        for n, f in enumerate(quad):
            select[:, f, n, r] = 1.0

    arrays = {"dense_ctx": inputs["dense_ctx"], "ids": inputs["ids"]}
    arrays.update({f"tbl_{f}": inputs[f"tbl_{f}"] for f in range(fields)})
    arrays.update({"w1a": w1a, "w1b": w1b, "select": select.reshape(3 * fields, 4 * rows), "ident": np.eye(128, dtype=np.float32),
                   "w1": w1, "w2": inputs["L0_rec_W2"], "wt1": inputs["W_top1"], "bt1": inputs["b_top1"],
                   "wt2": inputs["W_top2"], "bt2": inputs["b_top2"], "wt3": inputs["W_top3"]})
    nc = bacc.Bacc("TRN2", target_bir_lowering=False, num_devices=1)
    feeds, aps = {}, {}
    for name, a in arrays.items():
        a = np.ascontiguousarray(a)
        feeds[f"in_{name}"] = a
        aps[name] = nc.dram_tensor(f"in_{name}", a.shape, mybir.dt.from_np(a.dtype), kind="ExternalInput").ap()
    out = nc.dram_tensor("out_y", (batch, 1), mybir.dt.float32, kind="ExternalOutput").ap()
    build(nc, aps["dense_ctx"], aps["ids"], [aps[f"tbl_{f}"] for f in range(fields)], aps["w1a"], aps["w1b"],
          aps["select"], aps["ident"], aps["w1"], aps["w2"], aps["wt1"], aps["bt1"], aps["wt2"], aps["bt2"], aps["wt3"], out)
    result = run_bass_kernel_spmd(nc, [feeds], core_ids=[0])
    return result.results[0]["out_y"]
```
